# Optimizing a Trainium2 kernel written in Bass

```python
import numpy as np
import jax
import jax.numpy as jnp

def _softmax(x, axis=-1):
    return jax.nn.softmax(x, axis=axis)

def _gelu(x):
    return jax.nn.gelu(x, approximate=True)

def _silu(x):
    return jax.nn.silu(x)

def _sigmoid(x):
    return jax.nn.sigmoid(x)

def _layernorm(x, axis=-1, eps=1e-05):
    m = jnp.mean(x, axis=axis, keepdims=True)
    v = jnp.var(x, axis=axis, keepdims=True)
    return (x - m) / jnp.sqrt(v + eps)

def _scatter_add(tgt, idx, src, axis=0):
    return tgt.at[idx].add(src)

def _segment_sum(src, seg, n):
    return jax.ops.segment_sum(src, seg, n)
kernel_name = 'mk_prb_d2_jaxref_r4_923ec0'

def setup_inputs(seed: int=0):
    np.random.seed(seed)
    _w = jnp.asarray

    def _L0_attn_setup():
        import jax, jax.numpy as jnp
        import numpy as np
        B, T, D, H = (2, 512, 512, 16)
        DH = D // H
        ROPE_BASE = 10000.0

        def _rope(x, cos, sin):
            x0 = x[..., 0::2]
            x1 = x[..., 1::2]
            r0 = cos * x0 - sin * x1
            r1 = sin * x0 + cos * x1
            return jnp.stack((r0, r1), axis=-1).reshape(x.shape)
        key = jax.random.key(seed)
        ks = jax.random.split(key, 5)
        s = D ** (-0.5)
        return {'X': jax.random.normal(ks[0], (B, T, D), dtype=jnp.float32), 'Wq': jax.random.normal(ks[1], (D, D), dtype=jnp.float32) * s, 'Wk': jax.random.normal(ks[2], (D, D), dtype=jnp.float32) * s, 'Wv': jax.random.normal(ks[3], (D, D), dtype=jnp.float32) * s, 'Wo': jax.random.normal(ks[4], (D, D), dtype=jnp.float32) * s}
    _L0_attn_in = _L0_attn_setup()

    def _L0_ffn_setup():
        import jax, jax.numpy as jnp
        import numpy as np
        DIM_IN = 512
        DIM_HIDDEN = 2048
        key = jax.random.key(seed)
        k_x, k_g, k_u, k_d = jax.random.split(key, 4)
        s_in = 1.0 / np.sqrt(DIM_IN)
        s_hid = 1.0 / np.sqrt(DIM_HIDDEN)
        x = jax.random.normal(k_x, (4, 512, DIM_IN), dtype=jnp.float32)
        w_gate = jax.random.uniform(k_g, (DIM_HIDDEN, DIM_IN), jnp.float32, -s_in, s_in)
        w_up = jax.random.uniform(k_u, (DIM_HIDDEN, DIM_IN), jnp.float32, -s_in, s_in)
        w_down = jax.random.uniform(k_d, (DIM_IN, DIM_HIDDEN), jnp.float32, -s_hid, s_hid)
        return {'x': x, 'w_gate': w_gate, 'w_up': w_up, 'w_down': w_down}
    _L0_ffn_in = _L0_ffn_setup()

    def _L1_attn_setup():
        import jax, jax.numpy as jnp
        import numpy as np
        D_MODEL = 512
        N_HEADS = 16
        HEAD_DIM = D_MODEL // N_HEADS
        BATCH = 2
        SEQ = 512

        def apply_rope(x):
            b, h, t, d = x.shape
            half = d // 2
            pos = jnp.arange(t, dtype=x.dtype)[:, None]
            inv_freq = 1.0 / 10000.0 ** (jnp.arange(half, dtype=x.dtype) / half)
            angles = pos * inv_freq[None, :]
            sin = jnp.sin(angles)[None, None]
            cos = jnp.cos(angles)[None, None]
            x1, x2 = (x[..., :half], x[..., half:])
            return jnp.concatenate([x1 * cos - x2 * sin, x1 * sin + x2 * cos], axis=-1)
        key = jax.random.key(seed)
        ks = jax.random.split(key, 5)
        scale = 1.0 / np.sqrt(D_MODEL)
        x = jax.random.normal(ks[0], (BATCH, SEQ, D_MODEL), dtype=jnp.float32)
        Wq = jax.random.normal(ks[1], (D_MODEL, D_MODEL), dtype=jnp.float32) * scale
        Wk = jax.random.normal(ks[2], (D_MODEL, D_MODEL), dtype=jnp.float32) * scale
        Wv = jax.random.normal(ks[3], (D_MODEL, D_MODEL), dtype=jnp.float32) * scale
        Wo = jax.random.normal(ks[4], (D_MODEL, D_MODEL), dtype=jnp.float32) * scale
        return {'x': x, 'Wq': Wq, 'Wk': Wk, 'Wv': Wv, 'Wo': Wo}
    _L1_attn_in = _L1_attn_setup()

    def _L1_ffn_setup():
        import jax, jax.numpy as jnp
        import numpy as np
        HIDDEN = 512
        INTER = 1408
        B, S = (2, 512)

        def _ternary(key, shape):
            return jax.random.randint(key, shape, -1, 2).astype(jnp.float32)
        key = jax.random.key(seed)
        ks = jax.random.split(key, 7)
        x = jax.random.normal(ks[0], (B, S, HIDDEN), dtype=jnp.float32)
        gate_w = _ternary(ks[1], (INTER, HIDDEN))
        up_w = _ternary(ks[2], (INTER, HIDDEN))
        down_w = _ternary(ks[3], (HIDDEN, INTER))
        gate_s = jax.random.uniform(ks[4], (INTER,), minval=0.01, maxval=0.1, dtype=jnp.float32)
        up_s = jax.random.uniform(ks[5], (INTER,), minval=0.01, maxval=0.1, dtype=jnp.float32)
        down_s = jax.random.uniform(ks[6], (HIDDEN,), minval=0.01, maxval=0.1, dtype=jnp.float32)
        return {'x': x, 'gate_w': gate_w, 'up_w': up_w, 'down_w': down_w, 'gate_s': gate_s, 'up_s': up_s, 'down_s': down_s}
    _L1_ffn_in = _L1_ffn_setup()
    _d = {'L0_attn_X': _L0_attn_in['X'], 'L0_attn_Wq': _L0_attn_in['Wq'], 'L0_attn_Wk': _L0_attn_in['Wk'], 'L0_attn_Wv': _L0_attn_in['Wv'], 'L0_attn_Wo': _L0_attn_in['Wo'], 'L0_ffn_w_gate': _L0_ffn_in['w_gate'], 'L0_ffn_w_up': _L0_ffn_in['w_up'], 'L0_ffn_w_down': _L0_ffn_in['w_down'], 'L1_attn_Wq': _L1_attn_in['Wq'], 'L1_attn_Wk': _L1_attn_in['Wk'], 'L1_attn_Wv': _L1_attn_in['Wv'], 'L1_attn_Wo': _L1_attn_in['Wo'], 'L1_ffn_gate_w': _L1_ffn_in['gate_w'], 'L1_ffn_up_w': _L1_ffn_in['up_w'], 'L1_ffn_down_w': _L1_ffn_in['down_w'], 'L1_ffn_gate_s': _L1_ffn_in['gate_s'], 'L1_ffn_up_s': _L1_ffn_in['up_s'], 'L1_ffn_down_s': _L1_ffn_in['down_s']}
    _x0 = _d['L0_attn_X']
    _d['L0_attn_X'] = jax.random.normal(jax.random.fold_in(jax.random.key(seed), 1), (2, 1024, 512), dtype=_x0.dtype)
    del _x0
    return _d

def reference(L0_attn_X, L0_attn_Wq, L0_attn_Wk, L0_attn_Wv, L0_attn_Wo, L0_ffn_w_gate, L0_ffn_w_up, L0_ffn_w_down, L1_attn_Wq, L1_attn_Wk, L1_attn_Wv, L1_attn_Wo, L1_ffn_gate_w, L1_ffn_up_w, L1_ffn_down_w, L1_ffn_gate_s, L1_ffn_up_s, L1_ffn_down_s):

    def _L0_attn_ref(X, Wq, Wk, Wv, Wo):
        import jax, jax.numpy as jnp
        import numpy as np
        B, T, D, H = (2, 512, 512, 16)
        DH = D // H
        ROPE_BASE = 10000.0

        def _rope(x, cos, sin):
            x0 = x[..., 0::2]
            x1 = x[..., 1::2]
            r0 = cos * x0 - sin * x1
            r1 = sin * x0 + cos * x1
            return jnp.stack((r0, r1), axis=-1).reshape(x.shape)
        b, t, d = X.shape
        Q = X @ Wq.T
        K = X @ Wk.T
        V = X @ Wv.T
        Qh = Q.reshape(b, t, H, DH).transpose(0, 2, 1, 3)
        Kh = K.reshape(b, t, H, DH).transpose(0, 2, 1, 3)
        Vh = V.reshape(b, t, H, DH).transpose(0, 2, 1, 3)
        theta = ROPE_BASE ** (-2.0 * jnp.arange(DH // 2, dtype=jnp.float32) / DH)
        angles = jnp.arange(t, dtype=jnp.float32)[:, None] * theta[None, :]
        cos = jnp.cos(angles).astype(X.dtype)
        sin = jnp.sin(angles).astype(X.dtype)
        Qr = _rope(Qh, cos, sin)
        Kr = _rope(Kh, cos, sin)
        scores = jnp.einsum('bhqd,bhkd->bhqk', Qr, Kr) * DH ** (-0.5)
        causal = jnp.triu(jnp.ones((t, t), dtype=bool), 1)
        scores = jnp.where(causal, jnp.finfo(scores.dtype).min, scores)
        pattern = jax.nn.softmax(scores, axis=-1)
        heads = jnp.einsum('bhqk,bhkd->bqhd', pattern, Vh).reshape(b, t, d)
        return heads @ Wo.T

    def _L0_ffn_ref(x, w_gate, w_up, w_down):
        import jax, jax.numpy as jnp
        import numpy as np
        DIM_IN = 512
        DIM_HIDDEN = 2048
        gate = jnp.einsum('bsd,hd->bsh', x, w_gate)
        up = jnp.einsum('bsd,hd->bsh', x, w_up)
        gated = jax.nn.silu(gate) * up
        return jnp.einsum('bsh,dh->bsd', gated, w_down)

    def _L1_attn_ref(x, Wq, Wk, Wv, Wo):
        import jax, jax.numpy as jnp
        import numpy as np
        D_MODEL = 512
        N_HEADS = 16
        HEAD_DIM = D_MODEL // N_HEADS
        BATCH = 2
        SEQ = 512

        def apply_rope(x):
            b, h, t, d = x.shape
            half = d // 2
            pos = jnp.arange(t, dtype=x.dtype)[:, None]
            inv_freq = 1.0 / 10000.0 ** (jnp.arange(half, dtype=x.dtype) / half)
            angles = pos * inv_freq[None, :]
            sin = jnp.sin(angles)[None, None]
            cos = jnp.cos(angles)[None, None]
            x1, x2 = (x[..., :half], x[..., half:])
            return jnp.concatenate([x1 * cos - x2 * sin, x1 * sin + x2 * cos], axis=-1)
        b, t, _ = x.shape

        def proj(W):
            y = jnp.einsum('btd,ed->bte', x, W)
            return y.reshape(b, t, N_HEADS, HEAD_DIM).transpose(0, 2, 1, 3)
        q = apply_rope(proj(Wq))
        k = apply_rope(proj(Wk))
        v = proj(Wv)
        scores = jnp.einsum('bhqd,bhkd->bhqk', q, k) / np.sqrt(HEAD_DIM)
        causal = jnp.tril(jnp.ones((t, t), dtype=bool))
        scores = jnp.where(causal[None, None], scores, -jnp.inf)
        attn = jax.nn.softmax(scores, axis=-1)
        out = jnp.einsum('bhqk,bhkd->bhqd', attn, v)
        out = out.transpose(0, 2, 1, 3).reshape(b, t, D_MODEL)
        return jnp.einsum('btd,ed->bte', out, Wo)

    def _L1_ffn_ref(x, gate_w, up_w, down_w, gate_s, up_s, down_s):
        import jax, jax.numpy as jnp
        import numpy as np
        HIDDEN = 512
        INTER = 1408
        B, S = (2, 512)

        def _ternary(key, shape):
            return jax.random.randint(key, shape, -1, 2).astype(jnp.float32)
        b, s, h = x.shape
        xf = x.reshape(b * s, h)
        g = jnp.einsum('th,ih->ti', xf, gate_w) * gate_s
        u = jnp.einsum('th,ih->ti', xf, up_w) * up_s
        hdn = jax.nn.silu(g) * u
        out = jnp.einsum('ti,hi->th', hdn, down_w) * down_s
        return out.reshape(b, s, -1)
    x = L0_attn_X
    xn = _layernorm(x, axis=-1)
    x = x + _L0_attn_ref(xn, L0_attn_Wq, L0_attn_Wk, L0_attn_Wv, L0_attn_Wo) + _L0_ffn_ref(xn, L0_ffn_w_gate, L0_ffn_w_up, L0_ffn_w_down)
    xn = _layernorm(x, axis=-1)
    x = x + _L1_attn_ref(xn, L1_attn_Wq, L1_attn_Wk, L1_attn_Wv, L1_attn_Wo) + _L1_ffn_ref(xn, L1_ffn_gate_w, L1_ffn_up_w, L1_ffn_down_w, L1_ffn_gate_s, L1_ffn_up_s, L1_ffn_down_s)
    return x

_drawn_inputs = setup_inputs


def setup_inputs(seed=0):
    import zlib

    import numpy as np

    out = dict(_drawn_inputs(seed))
    spreads = {}
    factors = {}
    for name, (base, spread) in spreads.items():
        noise = np.random.default_rng([zlib.crc32(name.encode()), seed]).standard_normal(out[name].shape)
        drawn = base * np.exp(spread * noise) if base else spread * noise
        out[name] = jnp.asarray(drawn.astype(out[name].dtype))
    for name, factor in factors.items():
        out[name] = (out[name] * factor).astype(out[name].dtype)
    return out
```

```python
from contextlib import ExitStack

import concourse.bass as bass
from concourse import mybir

P = 128
B, T, D = 2, 1024, 512
H, DH = 16, 32
HG = P // DH
NG = H // HG
KC = D // P
RT = T // P
W = 512
NC = T // W
TPC = W // P
F0, F1 = 2048, 1408
CH = (F0 // P, F1 // P)
PAIRS = (2, 1)
EPS = 1e-5
SCALE = float(DH) ** -0.5
MASKED = -1e38
STACK = 3 * DH
SHIFT = STACK + 2

F32, F32R, BF16 = mybir.dt.float32, mybir.dt.float32r, mybir.dt.bfloat16
ALU = mybir.AluOpType
ACT = mybir.ActivationFunctionType
AX = mybir.AxisListType



NAT = [(qb, part, (min(qb + 1, TPC) if part == 0 else qb + 1 - TPC) * P)
       for qb in range(RT) for part in range(1 + (qb >= TPC))]
NATS = 3
SETS = [(c, kb) for c in range(NC) for kb in range(TPC * (c + 1))]


def mlp_pair(layer, j, nfc):
    out = []
    for blk in range(NC):
        for fc in range(nfc):
            last = blk == NC - 1 and fc == nfc - 1
            out.append([("gate", j, blk, fc, nfc)] + [("w", "G")] * last)
            out.append([("up", j, blk, fc, nfc), ("gated", j, blk, fc, nfc)] + [("w", "U")] * last)
        for half in range(2):
            last = blk == NC - 1 and half == 1
            add = ("add_down", "add_scaled")[layer]
            out.append([("down", j, blk, half, nfc), (add, j, blk, half, nfc)] + [("w", "D")] * last)
    return out


def attention():
    out = [[("v_slice",)]]
    out += [[("proj", t)] for t in range(2 * NC)]
    out[-1].append(("w", "A"))
    nat = [[("nat", h, u)] for h in range(HG) for u in range(0, len(NAT), NATS)]
    st = []
    for i, (c, kb) in enumerate(SETS):
        st.append([("st", i)] + ([("pv", i - 1)] if i and kb else []))
        if kb == TPC * (c + 1) - 1:
            st.append([("pv", i), ("heads", c)])
    wo = [[("wo", c), ("add_wo", c)] for c in range(NC)]
    wo[-1].append(("w", "O"))
    return out, nat, st, wo


def turn(layer):
    mlp = [p for j in range(PAIRS[layer]) for p in mlp_pair(layer, j, 2)]
    proj, nat, st, wo = attention()
    first = st[:TPC + 1]
    second = st[TPC + 1:]
    out = []
    n = len(mlp)
    out += proj
    fill = mlp[:2]
    rest = mlp[2:]
    out += fill
    k = (n - 2) // 2
    here, rest = rest[:k], rest[k:]
    out += merged(nat, here)
    out += [[("shift",)]]
    k = min(2, len(rest))
    out += rest[:k]
    rest = rest[k:]
    out += merged(first + second[:1] + wo[:1] + second[1:], rest)
    out += wo[1:]
    return [s for piece in out for s in piece]


def merged(a, b):
    out, k = [], 0
    for i, piece in enumerate(a):
        out.append(piece)
        while k < len(b) and (k + 1) * len(a) <= (i + 1) * len(b):
            out.append(b[k])
            k += 1
    return out + b[k:]


def opening(layer):
    out = [("v_weights",), ("stats",)]
    for rt in range(RT):
        out += [("norm", rt)] + ([("values", rt - 1)] if rt else [])
    return out + [("values", RT - 1)]


def closing(layer):
    left = CH[layer] - NG * 2 * PAIRS[layer]
    out = []
    for j, nfc in enumerate([2] * (left // 2) + [1] * (left % 2)):
        out += [s for piece in mlp_pair(layer, PAIRS[layer] + j, nfc) for s in piece]
    return out


ADDS = {
    "v_weights": {"d_wv": 16, "d_rope": 16, "v_wv": 1, "g_wv": 1},
    "stats": {"v_chain": 2 * RT + 5, "v_var": 1, "a_std": 1},
    "norm": {"v_xn": 1, "p_xt": 1, "a_xh": 1, "v_dfree": 1},
    "values": {"p_v": 1, "v_dfree": 1},
    "v_slice": {"d_v": 16},
    "proj": {"p_proj": 1, "v_pfree": 1, "v_chain": 2, "v_rope": 1, "a_rh": 1, "v_rl": 1},
    "nat": {"p_nat": NATS, "v_max": NATS},
    "shift": {"v_chain": 2, "v_m": 1, "p_shift": 1, "v_shift": 1, "d_shift": 32},
    "st": {"p_st": HG, "a_exp": HG},
    "pv": {"p_pv": 1},
    "heads": {"a_heads": 1, "v_chain": 3, "v_heads": 1},
    "wo": {"p_wo": TPC},
    "add_wo": {"v_dfree": TPC},
    "gate": {"p_gate": 1, "a_tanh": 1},
    "up": {"p_up": 1},
    "gated": {"v_gate": 1, "v_h": 1, "a_hh": 1, "g_hl": 1},
    "down": {"p_down": TPC // 2},
    "add_down": {"v_dfree": TPC // 2},
    "add_scaled": {"v_scaled": TPC // 2, "v_dfree": TPC // 2},
    "w": {"v_hi": 1, "g_lo": 1},
}
STACKS = 3 * HG * 16

SPLITS = (
    [("A", 0, "U", 2), ("G", 1, "D", 2), ("U", 0, "G", 4), ("D", 1, "U", 4),
     ("G", 0, "D", 4), ("U", 1, "O", 1), ("D", 0, "A", 2), ("O", 1, "G", 6)],
    [("A", 0, "U", 2), ("G", 1, "D", 2), ("U", 0, "O", 1), ("D", 1, "G", 4), ("O", 0, "A", 2)],
)
SPLITS_CLOSE = [("G", 1, "U", 26), ("U", 1, "D", 26), ("D", 1, "G", 27),
                ("G", 1, "U", 27), ("U", 1, "D", 27), ("D", 1, "G", 29)]
SPLITS_OPEN = [("A", 0), ("O", 1), ("G", 0), ("U", 1), ("D", 0)]

SEMS = sorted({x for a in ADDS.values() for x in a} | {"raw0", "raw1", "d_stack0", "d_stack1", "d_x", "d_out"})
CREDIT = {s: 0 if s[0] == "d" or s[:3] == "raw" else 1 for s in SEMS}
CREDIT.update(v_dfree=2, g_hl=2, d_out=16, d_stack0=16, d_stack1=16)


def splits_of(region):
    return {"turn0": SPLITS[0], "turn1": SPLITS[1], "close": SPLITS_CLOSE}.get(region, [])


class Count:

    def __init__(self):
        self.n = dict(CREDIT)
        self.n["v_hi"] += len(SPLITS_OPEN)
        self.n["g_lo"] += len(SPLITS_OPEN)
        for _, slot in SPLITS_OPEN:
            self.n[f"raw{slot}"] += 16
        self.loops = []
        self.bases = {}
        self.split = 0
        self.d = 0

    def dk(self):
        self.d += 1
        return (self.d - 1) % 2

    def ready(self, kind):
        return self.base("g_lo") + self.w_ready[kind]

    def __call__(self, sem, k=0):
        return self.base(sem) + (self.n[sem] + k)

    def base(self, sem):
        if sem not in self.bases:
            v = 0
            for i, per in self.loops:
                v = i * per[sem] + v
            self.bases[sem] = self.eng.snap(v)
        return self.bases[sem]

    def did(self, step, region):
        for sem, k in ADDS[step[0]].items():
            self.n[sem] += k
        if step[0] == "proj":
            self.n[f"d_stack{step[1] % 2}"] += STACKS
        if step[0] == "w":
            self.n[f"raw{splits_of(region)[self.split][1]}"] += 16
            self.split += 1
        if step == ("stats",) and region == "open0":
            self.n["d_x"] += 16
        if step == ("store",):
            self.n["d_out"] += 16


ADDS["store"] = {}


def total(parts):
    c = Count()
    before = dict(c.n)
    for region, steps, times in parts:
        for _ in range(times):
            c.split = 0
            for s in steps:
                c.did(s, region)
    return {k: c.n[k] - before[k] for k in c.n}


REGIONS = []
for _l in (0, 1):
    REGIONS += [(f"open{_l}", opening(_l), 1), (f"turn{_l}", turn(_l), NG)]
REGIONS += [("close", closing(1) + [("store",)], 1)]
LAYER = {"open0": 0, "turn0": 0, "open1": 1, "turn1": 1, "close": 1}
PER_BATCH = total(REGIONS)


def two_layers(nc, x, wqk, wo, wv, wgate, wup, wdown, rope, scales, down_s, out):
    ctx = ExitStack()
    with ctx:
        def sb(name, shape, dt=F32):
            return ctx.enter_context(nc.sbuf_tensor(name, shape, dt))

        def bank(name):
            return ctx.enter_context(nc.psum_tensor(name, [P, W], F32))

        sem = {s: ctx.enter_context(nc.semaphore(s)) for s in SEMS}
        s_const = ctx.enter_context(nc.semaphore("s_const"))
        d_const = ctx.enter_context(nc.semaphore("d_const"))
        s_vconst = ctx.enter_context(nc.semaphore("s_vconst"))

        xres = sb("xres", [P, RT, D])
        xh, xl = sb("xh", [P, KC, T], F32R), sb("xl", [P, KC, T], F32R)
        val = sb("val", [P, RT, D])
        vh = sb("vh", [P, RT, P])
        raw = sb("raw", [P, 2, 2 * W])
        wqkh, wqkl = sb("wqkh", [P, 2, KC, P], F32R), sb("wqkl", [P, 2, KC, P], F32R)
        woh, wol = sb("woh", [P, D], F32R), sb("wol", [P, D], F32R)
        wgh, wgl = sb("wgh", [P, 2, KC, P], F32R), sb("wgl", [P, 2, KC, P], F32R)
        wuh, wul = sb("wuh", [P, 2, KC, P], F32R), sb("wul", [P, 2, KC, P], F32R)
        wdh, wdl = sb("wdh", [P, 2, D], F32R), sb("wdl", [P, 2, D], F32R)
        QS, KS = sb("QS", [P, HG, T], F32R), sb("KS", [P, HG, T], F32R)
        wvh = QS[:, 0:2, :].rearrange("p a (b n) -> p (a b) n", n=D)
        wvl = QS[:, 2:4, :].rearrange("p a (b n) -> p (a b) n", n=D)
        flat_h, flat_l = sb("flat_h", [P, 2, W], F32R), sb("flat_l", [P, 2, W], F32R)
        swapped, turned = sb("swapped", [P, W]), sb("turned", [P, W])
        trig = sb("trig", [P, 2, T])
        pr = sb("pr", [P, 8, W])
        wv_raw = pr[:, 0:KC, :]
        xn = pr[:, KC:KC + 2, :]
        heads, denom = sb("heads", [P, W]), sb("denom", [P, W])
        ah, al = sb("ah", [P, W], F32R), sb("al", [P, W], F32R)
        tt = sb("tt", [P, 2, W])
        hh, hl = sb("hh", [P, 2, W], F32R), sb("hl", [P, 2, W], F32R)
        ds = sb("ds", [P, D])
        ident = sb("ident", [P, P])
        ident_b = sb("ident_b", [P, P], BF16)
        mask_q, mask_k = sb("mask_q", [P, P], BF16), sb("mask_k", [P, P], BF16)
        ones = sb("ones", [P, DH])
        mp = sb("mp", [P, HG * RT, 2])
        mx = sb("mx", [P, HG * RT])
        mm = sb("mm", [P, P // (HG * RT), HG * RT])
        mt = sb("mt", [2 * HG * RT, P], F32R)
        stat6 = sb("stat6", [P, RT, 6])
        mv = sb("mv", [P, RT, 2])
        st = sb("st", [P, 6, RT])
        sc = sb("sc", [P, CH[1], 2])
        half_gs, both_s = sb("half_gs", [P, CH[1]]), sb("both_s", [P, CH[1]])

        S = [bank("S0"), bank("S1")]
        G, U = bank("G"), bank("U")
        Dk = [bank("D0"), bank("D1")]
        O, E = bank("O"), bank("E")

        SPLIT_TO = {"A": (wqkh, wqkl), "O": (woh, wol), "G": (wgh, wgl), "U": (wuh, wul), "D": (wdh, wdl)}
        SIZE = {"A": 2 * W, "O": W, "G": 2 * W, "U": 2 * W, "D": 2 * W}
        FREED_BY = {"A": "p_proj", "O": "p_wo", "G": "p_gate", "U": "p_up", "D": "p_down"}

        def flat(t):
            return t[:, :] if len(t.shape) == 2 else t[:, :, :].rearrange("p a b -> p (a b)") \
                if len(t.shape) == 3 else t[:, :, :, :].rearrange("p a b c -> p (a b c)")

        def load(sp, kind, at, slot):
            dst = raw[:, slot, 0:SIZE[kind]]
            if kind in "AO":
                src = (wqk if kind == "A" else wo)[bass.ds(at, 1), :, :].rearrange("a p n -> p (a n)")
            else:
                src = {"G": wgate, "U": wup, "D": wdown}[kind][bass.ds(at, 2), :, :].rearrange("a p n -> p a n")
                dst = dst.rearrange("p (a n) -> p a n", a=2)
            sp.dma_start(dst, src).then_inc(sem[f"raw{slot}"], 16)

        def walk(eng, part):
            with eng.Fori(0, B) as b:
                n = Count()
                n.eng, n.b = eng, b
                n.loops.append((b, PER_BATCH))
                n.part = part
                for region, steps, times in REGIONS:
                    n.region, n.layer = region, LAYER[region]
                    n.split, n.d, n.turns = 0, 0, NG - 1
                    n.w_ready = {"A": n.n["g_lo"] - 4, "O": n.n["g_lo"], "G": n.n["g_lo"] - 2,
                                 "U": n.n["g_lo"] - 1, "D": n.n["g_lo"]}
                    n.bases = {}
                    if times == 1:
                        walk_steps(n, steps)
                        continue
                    start = dict(n.n)
                    with eng.Fori(0, times) as g:
                        per = total([(region, steps, 1)])
                        n.loops.append((g, per))
                        n.bases = {}
                        n.turns = g
                        walk_steps(n, steps)
                        n.loops.pop()
                    for k in start:
                        n.n[k] = start[k] + times * (n.n[k] - start[k])

        def walk_steps(n, steps):
            for s in steps:
                if s[0] in n.part:
                    n.part[s[0]](n, *s[1:])
                n.did(s, n.region)
                if s[0] == "w":
                    n.w_ready[s[1]] = n.n["g_lo"]

        def chunk(n, j, fc):
            at = n.turns * (2 * PAIRS[1]) + (2 * j + fc)
            return bass.ds(at, 1)

        block = ctx.enter_context(nc.Block())

        @block.sync
        def _(sp):
            for s in SEMS:
                if CREDIT[s]:
                    sp.sem_inc(sem[s], CREDIT[s])
            sp.dma_start(sc[:, :, :], scales).then_inc(d_const, 16)
            sp.dma_start(ds[:, :], down_s).then_inc(d_const, 16)
            for i, (kind, slot) in enumerate(SPLITS_OPEN):
                if i >= 2:
                    sp.wait_ge(sem["g_lo"], CREDIT["g_lo"] + i - 1)
                load(sp, kind, 0, slot)
            sp.wait_ge(sem["g_lo"], CREDIT["g_lo"] + 4)
            load(sp, "G", 2, 1)
            sp.wait_ge(sem["g_lo"], CREDIT["g_lo"] + 5)
            load(sp, "A", 1, 0)

            def v_weights(n):
                sp.wait_ge(sem["p_pv"], n("p_pv"))
                sp.dma_start(wv_raw, wv[n.layer].rearrange("p (c n) -> p c n", c=KC)).then_inc(sem["d_wv"], 16)
                sp.wait_ge(sem["v_rl"], n("v_rl"))
                sp.dma_start(trig[:, :, :], rope[n.layer]).then_inc(sem["d_rope"], 16)

            def stats(n):
                if n.layer == 0:
                    sp.wait_ge(sem["d_out"], n("d_out"))
                    sp.dma_start(xres[:, :, :], x[bass.ds(n.b, 1), :, :].rearrange("a (t p) d -> p (a t) d", p=P)) \
                        .then_inc(sem["d_x"], 16)

            def v_slice(n):
                sp.wait_ge(sem["v_dfree"], n("v_dfree"))
                sp.wait_ge(sem["p_pv"], n("p_pv"))
                sp.dma_start(vh[:, :, :], val[:, :, bass.ds(n.turns * P, P)]).then_inc(sem["d_v"], 16)

            def proj(n, t):
                par, c = t % 2, t % NC
                parts = [(KS, (flat_h, flat_h, flat_l)), (QS, (flat_h, flat_l, flat_h))][t // NC]
                sp.wait_ge(sem["v_rl"], n("v_rl", 1))
                for h in range(HG):
                    for r, src in enumerate(parts[1]):
                        sp.dma_start(parts[0][r * DH:(r + 1) * DH, h, c * W:(c + 1) * W].bitcast(F32),
                                     src[h * DH:(h + 1) * DH, par, :].bitcast(F32)).then_inc(sem[f"d_stack{par}"], 16)

            def shift(n):
                sp.wait_ge(sem["v_shift"], n("v_shift", 1))
                for k in range(2):
                    sp.dma_start(QS[STACK + k:STACK + k + 1, :, :].rearrange("o h (q n) -> o (h q) n", n=P).bitcast(F32),
                                 mt[k * HG * RT:(k + 1) * HG * RT, :].bitcast(F32)).then_inc(sem["d_shift"], 16)

            def w(n, kind):
                _, slot, nxt, ahead = splits_of(n.region)[n.split]
                sp.wait_ge(sem["g_lo"], n("g_lo", 1))
                if n.region == "close":
                    at = ahead
                elif nxt in "AO":
                    at = n.turns + (NG * n.layer + ahead)
                else:
                    at = n.turns * (2 * PAIRS[n.layer]) + (CH[0] * n.layer + ahead)
                load(sp, nxt, at, slot)

            def store(n):
                sp.wait_ge(sem["v_dfree"], n("v_dfree"))
                sp.dma_start(out[bass.ds(n.b, 1), :, :].rearrange("a (t p) d -> p (a t) d", p=P), xres[:, :, :]) \
                    .then_inc(sem["d_out"], 16)

            walk(sp, dict(v_weights=v_weights, stats=stats, v_slice=v_slice, proj=proj, shift=shift, w=w, store=store))
            sp.wait_ge(sem["d_out"], CREDIT["d_out"] + 16 * B)
            for k in range(2):
                sp.wait_ge(sem[f"raw{k}"], 16 * sum(s == k for _, s in SPLITS_OPEN) + B * PER_BATCH[f"raw{k}"] + 16)

        @block.scalar
        def _(act):
            def stats(n):
                act.wait_ge(sem["v_var"], n("v_var", 1))
                act.activation(st[:, 1, :], st[:, 0, :], ACT.Sqrt).then_inc(sem["a_std"], 1)

            def norm(n, rt):
                act.wait_ge(sem["p_xt"], n("p_xt", 1))
                bank_ = Dk[n.dk()]
                act.copy(xh[:, :, rt * P:(rt + 1) * P], bank_[:, :].rearrange("p (c n) -> p c n", c=KC)) \
                    .then_inc(sem["a_xh"], 1)

            def values(n, rt):
                n.dk()

            def proj(n, t):
                act.wait_ge(sem["v_rope"], n("v_rope", 1))
                act.wait_ge(sem[f"d_stack{t % 2}"], n(f"d_stack{t % 2}"))
                act.copy(flat_h[:, t % 2, :], turned[:, :]).then_inc(sem["a_rh"], 1)

            def st_(n, i):
                c, kb = SETS[i]
                w_ = W - max(0, kb - TPC * c) * P
                act.wait_ge(sem["p_pv"], n("p_pv") if i == 0 or kb else n("p_pv", -1))
                for h in range(HG):
                    act.wait_ge(sem["p_st"], n("p_st", h + 1))
                    act.activation(pr[:, (i * HG + h) % 8, W - w_:], S[h % 2][:, W - w_:], ACT.Exp, scale=SCALE) \
                        .then_inc(sem["a_exp"], 1)

            def heads_(n, c):
                act.wait_ge(sem["p_pv"], n("p_pv"))
                act.wait_ge(sem["v_heads"], n("v_heads"))
                act.copy(heads[:, :], O[:, :])
                act.copy(denom[:, :], E[:, :]).then_inc(sem["a_heads"], 1)

            def gate(n, j, blk, fc, nfc):
                act.wait_ge(sem["p_gate"], n("p_gate", 1))
                act.wait_ge(sem["g_hl"], n("g_hl", -1))
                par = (blk * nfc + fc) % 2
                act.activation(tt[:, par, :], G[:, :], ACT.Tanh,
                               scale=half_gs[:, chunk(n, j, fc)] if n.layer else 0.5).then_inc(sem["a_tanh"], 1)

            def gated(n, j, blk, fc, nfc):
                act.wait_ge(sem["v_h"], n("v_h", 1))
                act.wait_ge(sem["p_down"], n("p_down"))
                act.copy(hh[:, fc, :], tt[:, (blk * nfc + fc) % 2, :]).then_inc(sem["a_hh"], 1)

            act.wait_ge(s_vconst, 2)
            walk(act, dict(stats=stats, norm=norm, values=values, proj=proj, st=st_, heads=heads_, gate=gate, gated=gated))

        @block.gpsimd
        def _(pool):
            pool.memset(ident[:, :], 1.0).then_inc(s_const, 1)
            pool.memset(ident_b[:, :], 1.0).then_inc(s_const, 1)
            pool.memset(mask_q[:, :], 0.0).then_inc(s_const, 1)
            pool.memset(mask_k[:, :], 0.0).then_inc(s_const, 1)
            pool.wait_ge(s_const, 4)
            for t in (ident, ident_b):
                pool.affine_select(out=t[:, :], in_=t[:, :], pattern=[[1, P]], compare_op=ALU.is_equal, fill=0.0,
                                   base=0, channel_multiplier=-1).then_inc(s_const, 1)
            pool.affine_select(out=mask_q[:, :], in_=mask_q[:, :], pattern=[[-1, P]], compare_op=ALU.is_ge,
                               fill=MASKED, base=0, channel_multiplier=1).then_inc(s_const, 1)
            pool.affine_select(out=mask_k[:, :], in_=mask_k[:, :], pattern=[[1, P]], compare_op=ALU.is_ge,
                               fill=MASKED, base=0, channel_multiplier=-1).then_inc(s_const, 1)

            def low(kind, slot):
                hi, lo = SPLIT_TO[kind]
                return pool.tensor_tensor(flat(lo), raw[:, slot, 0:SIZE[kind]], flat(hi).bitcast(F32), ALU.subtract)

            for i, (kind, slot) in enumerate(SPLITS_OPEN):
                pool.wait_ge(sem["v_hi"], CREDIT["v_hi"] + i + 1)
                low(kind, slot).then_inc(sem["g_lo"], 1)

            def v_weights(n):
                pool.wait_ge(sem["v_wv"], n("v_wv", 1))
                pool.tensor_tensor(wvl, wv_raw, wvh.bitcast(F32), ALU.subtract).then_inc(sem["g_wv"], 1)

            def w(n, kind):
                pool.wait_ge(sem["v_hi"], n("v_hi", 1))
                low(kind, splits_of(n.region)[n.split][1]).then_inc(sem["g_lo"], 1)

            def gated(n, j, blk, fc, nfc):
                pool.wait_ge(sem["a_hh"], n("a_hh", 1))
                pool.tensor_tensor(hl[:, fc, :], tt[:, (blk * nfc + fc) % 2, :], hh[:, fc, :].bitcast(F32), ALU.subtract) \
                    .then_inc(sem["g_hl"], 1)

            walk(pool, dict(v_weights=v_weights, w=w, gated=gated))

        @block.vector
        def _(dve):
            def high(kind, slot):
                return dve.tensor_copy(flat(SPLIT_TO[kind][0]), raw[:, slot, 0:SIZE[kind]])

            dve.memset(ones[:, :], 1.0)
            dve.memset(mp[:, :, :], -3e38)
            dve.memset(mm[:, :, :], 0.0)
            dve.memset(KS[STACK:P, :, :].bitcast(F32), 1.0)
            dve.wait_ge(d_const, 32)
            dve.tensor_scalar(half_gs[:, :], sc[:, :, 0], 0.5, None, ALU.mult).then_inc(s_vconst, 1)
            dve.wait_ge(s_vconst, 1)
            dve.tensor_tensor(both_s[:, :], half_gs[:, :], sc[:, :, 1], ALU.mult).then_inc(s_vconst, 1)
            dve.wait_ge(s_vconst, 2)
            opened = {0: 0, 1: 0}
            for kind, slot in SPLITS_OPEN:
                opened[slot] += 16
                dve.wait_ge(sem[f"raw{slot}"], opened[slot])
                high(kind, slot).then_inc(sem["v_hi"], 1)

            def linker(n):
                k = [0]

                def link(ins):
                    k[0] += 1
                    ins.then_inc(sem["v_chain"], 1)
                    dve.wait_ge(sem["v_chain"], n("v_chain", k[0]))
                return link

            def v_weights(n):
                dve.wait_ge(sem["d_wv"], n("d_wv", 16))
                dve.wait_ge(sem["p_st"], n("p_st"))
                dve.tensor_copy(wvh, wv_raw).then_inc(sem["v_wv"], 1)

            def stats(n):
                link = linker(n)
                if n.layer == 0:
                    dve.wait_ge(sem["d_x"], n("d_x", 16))
                else:
                    dve.wait_ge(sem["v_dfree"], n("v_dfree"))
                for rt in range(RT):
                    dve.bn_stats(stat6[:, rt, :], xres[:, rt, :]).then_inc(sem["v_chain"], 1)
                dve.wait_ge(sem["v_chain"], n("v_chain", RT))
                dve.memset(st[:, 2, :], 0.0)
                for rt in range(RT):
                    dve.bn_aggr(mv[:, rt, :], stat6[:, rt, :]).then_inc(sem["v_chain"], 1)
                dve.wait_ge(sem["v_chain"], n("v_chain", 2 * RT))
                dve.tensor_scalar(st[:, 0, :], mv[:, :, 1], EPS, None, ALU.add).then_inc(sem["v_var"], 1)
                dve.wait_ge(sem["v_var"], n("v_var", 1))
                dve.wait_ge(sem["a_std"], n("a_std", 1))
                k = 2 * RT

                def step(ins):
                    nonlocal k
                    k += 1
                    ins.then_inc(sem["v_chain"], 1)
                    dve.wait_ge(sem["v_chain"], n("v_chain", k))
                step(dve.reciprocal(st[:, 2, :], st[:, 1, :]))
                step(dve.tensor_tensor(st[:, 3, :], st[:, 0, :], st[:, 2, :], ALU.mult))
                step(dve.tensor_tensor(st[:, 4, :], st[:, 3, :], st[:, 1, :], ALU.add))
                step(dve.reciprocal(st[:, 3, :], st[:, 4, :]))
                step(dve.tensor_scalar(st[:, 5, :], st[:, 3, :], 2.0, None, ALU.mult))

            def norm(n, rt):
                if rt >= 2:
                    dve.wait_ge(sem["p_xt"], n("p_xt", -1))
                else:
                    dve.wait_ge(sem["p_pv"], n("p_pv"))
                    dve.wait_ge(sem["p_xt"], n("p_xt"))
                dve.tensor_scalar(xn[:, rt % 2, :], xres[:, rt, :], mv[:, rt, 0:1], st[:, 5, rt:rt + 1],
                                  ALU.subtract, ALU.mult).then_inc(sem["v_xn"], 1)
                dve.wait_ge(sem["a_xh"], n("a_xh", 1))
                dve.tensor_tensor(xl[:, :, rt * P:(rt + 1) * P],
                                  Dk[n.dk()][:, :].rearrange("p (c n) -> p c n", c=KC),
                                  xh[:, :, rt * P:(rt + 1) * P].bitcast(F32), ALU.subtract) \
                    .then_inc(sem["v_dfree"], 1)

            def values(n, rt):
                dve.wait_ge(sem["p_v"], n("p_v", 1))
                dve.tensor_copy(val[:, rt, :], Dk[n.dk()][:, :]).then_inc(sem["v_dfree"], 1)

            def proj(n, t):
                link = linker(n)
                cols = slice((t % NC) * W, (t % NC + 1) * W)
                if t == 0:
                    dve.wait_ge(sem["d_rope"], n("d_rope"))
                dve.wait_ge(sem["p_proj"], n("p_proj", 1))
                dve.wait_ge(sem["v_rl"], n("v_rl"))
                dve.wait_ge(sem["a_rh"], n("a_rh"))
                dve.tensor_tensor(turned[:, :], S[t % 2][:, :], trig[:, 0, cols], ALU.mult).then_inc(sem["v_pfree"], 1)
                dve.stream_shuffle(swapped[:, :], S[t % 2][:, :], [i ^ 1 for i in range(32)]) \
                    .then_inc(sem["v_chain"], 1)
                dve.wait_ge(sem["v_chain"], n("v_chain", 1))
                dve.tensor_tensor(swapped[:, :], swapped[:, :], trig[:, 1, cols], ALU.mult).then_inc(sem["v_chain"], 1)
                dve.wait_ge(sem["v_chain"], n("v_chain", 2))
                dve.wait_ge(sem["v_pfree"], n("v_pfree", 1))
                dve.tensor_tensor(turned[:, :], turned[:, :], swapped[:, :], ALU.add).then_inc(sem["v_rope"], 1)
                dve.wait_ge(sem["v_rope"], n("v_rope", 1))
                dve.wait_ge(sem["a_rh"], n("a_rh", 1))
                dve.tensor_tensor(flat_l[:, t % 2, :], turned[:, :], flat_h[:, t % 2, :].bitcast(F32), ALU.subtract) \
                    .then_inc(sem["v_rl"], 1)

            def nat(n, h, u0):
                for i in range(NATS):
                    qb, part, w_ = NAT[u0 + i]
                    dve.wait_ge(sem["p_nat"], n("p_nat", i + 1))
                    at = h * RT + qb
                    dve.tensor_reduce(mp[:, at, part:part + 1], S[(u0 + i) % 2][:, 0:w_], AX.X, ALU.max) \
                        .then_inc(sem["v_max"], 1)

            def shift(n):
                link = linker(n)
                dve.wait_ge(sem["v_max"], n("v_max"))
                link(dve.tensor_reduce(mx[:, :], mp[:, :, :], AX.X, ALU.max))
                link(dve.tensor_scalar(mm[:, 0, :].bitcast(F32R), mx[:, :], -1.0, None, ALU.mult))
                dve.scalar_tensor_tensor(mm[:, 1, :], mx[:, :], -1.0, mm[:, 0, :], ALU.mult, ALU.subtract) \
                    .then_inc(sem["v_m"], 1)
                dve.wait_ge(sem["p_shift"], n("p_shift", 1))
                dve.tensor_copy(mt[:, :], E[0:2 * HG * RT, 0:P]).then_inc(sem["v_shift"], 1)

            def heads_(n, c):
                link = linker(n)
                dve.wait_ge(sem["a_heads"], n("a_heads", 1))
                link(dve.reciprocal(denom[:, :], denom[:, :]))
                link(dve.tensor_tensor(heads[:, :], heads[:, :], denom[:, :], ALU.mult))
                dve.wait_ge(sem["p_wo"], n("p_wo"))
                link(dve.tensor_copy(ah[:, :], heads[:, :]))
                dve.tensor_tensor(al[:, :], heads[:, :], ah[:, :].bitcast(F32), ALU.subtract) \
                    .then_inc(sem["v_heads"], 1)

            def add_wo(n, c):
                for i in range(TPC):
                    dve.wait_ge(sem["p_wo"], n("p_wo", i + 1 - TPC))
                    dve.wait_ge(sem["v_dfree"], n("v_dfree", i))
                    rt = c * TPC + i
                    dve.tensor_tensor(xres[:, rt, :], Dk[n.dk()][:, :], xres[:, rt, :], ALU.add) \
                        .then_inc(sem["v_dfree"], 1)

            def add_down(n, j, blk, half, nfc):
                for i in range(TPC // 2):
                    rt = blk * TPC + half * (TPC // 2) + i
                    dve.wait_ge(sem["p_down"], n("p_down", i + 1 - TPC // 2))
                    dve.wait_ge(sem["v_dfree"], n("v_dfree", i))
                    d = Dk[n.dk()]
                    if n.layer:
                        dve.tensor_tensor(d[:, :], d[:, :], ds[:, :], ALU.mult).then_inc(sem["v_scaled"], 1)
                        dve.wait_ge(sem["v_scaled"], n("v_scaled", i + 1))
                    dve.tensor_tensor(xres[:, rt, :], d[:, :], xres[:, rt, :], ALU.add).then_inc(sem["v_dfree"], 1)

            def gated(n, j, blk, fc, nfc):
                t = tt[:, (blk * nfc + fc) % 2, :]
                dve.wait_ge(sem["a_tanh"], n("a_tanh"))
                dve.scalar_tensor_tensor(t, t, 1.0, G[:, :], ALU.add, ALU.mult).then_inc(sem["v_gate"], 1)
                dve.wait_ge(sem["v_gate"], n("v_gate", 1))
                dve.wait_ge(sem["p_up"], n("p_up"))
                dve.scalar_tensor_tensor(t, t, both_s[:, chunk(n, j, fc)] if n.layer else 0.5, U[:, :],
                                         ALU.mult, ALU.mult).then_inc(sem["v_h"], 1)

            def w(n, kind):
                slot = splits_of(n.region)[n.split][1]
                dve.wait_ge(sem[f"raw{slot}"], n(f"raw{slot}", 16))
                dve.wait_ge(sem[FREED_BY[kind]], n(FREED_BY[kind]))
                high(kind, slot).then_inc(sem["v_hi"], 1)

            walk(dve, dict(v_weights=v_weights, stats=stats, norm=norm, values=values, proj=proj, nat=nat, shift=shift,
                           heads=heads_, add_wo=add_wo, add_down=add_down, add_scaled=add_down, gated=gated, w=w))

        @block.tensor
        def _(pe):
            pe.wait_ge(s_const, 8)
            pe.wait_ge(s_vconst, 2)

            def three(dst, terms, start=True, stop=True):
                seq = [m for (ah_, al_), (bh, bl) in terms for m in ((ah_, bh), (ah_, bl), (al_, bh))]
                for i, (a, b_) in enumerate(seq):
                    ins = pe.matmul(dst, a, b_, start=i == 0, stop=i == len(seq) - 1)
                return ins

            def norm(n, rt):
                pe.wait_ge(sem["v_xn"], n("v_xn", 1))
                pe.wait_ge(sem["v_dfree"], n("v_dfree", -1))
                d = Dk[n.dk()]
                for c in range(KC):
                    ins = pe.transpose(d[:, c * P:(c + 1) * P], xn[:, rt % 2, c * P:(c + 1) * P], ident[:, :])
                ins.then_inc(sem["p_xt"], 1)

            def values(n, rt):
                if rt == 0:
                    pe.wait_ge(sem["g_wv"], n("g_wv"))
                pe.wait_ge(sem["v_dfree"], n("v_dfree", -1))
                d = Dk[n.dk()]
                rows = slice(rt * P, (rt + 1) * P)
                three(d[:, :], [((xh[:, c, rows], xl[:, c, rows]), (wvh[:, c, :], wvl[:, c, :])) for c in range(KC)]) \
                    .then_inc(sem["p_v"], 1)

            def proj(n, t):
                if t == 0:
                    pe.wait_ge(sem["g_lo"], n.ready("A"))
                    pe.wait_ge(sem["v_dfree"], n("v_dfree"))
                if t < 2:
                    pe.wait_ge(sem["a_exp"], n("a_exp"))
                else:
                    pe.wait_ge(sem["v_rope"], n("v_rope", -1))
                cols = slice((t % NC) * W, (t % NC + 1) * W)
                qk = 1 - t // NC
                three(S[t % 2][:, :], [((wqkh[:, qk, c, :], wqkl[:, qk, c, :]), (xh[:, c, cols], xl[:, c, cols]))
                                       for c in range(KC)]).then_inc(sem["p_proj"], 1)

            def nat(n, h, u0):
                if h == 0 and u0 == 0:
                    for k in range(2):
                        pe.wait_ge(sem[f"d_stack{k}"], n(f"d_stack{k}"))
                for i in range(NATS):
                    qb, part, w_ = NAT[u0 + i]
                    if not (h == 0 and u0 + i < 2):
                        pe.wait_ge(sem["v_max"], n("v_max", i - 1))
                    k0 = part * W
                    diag = qb * P - k0
                    s = S[(u0 + i) % 2]
                    wide = max(w_, 2 * P)
                    masked = diag == w_ - P
                    ins = pe.matmul(s[:, 0:wide], QS[0:STACK, h, qb * P:(qb + 1) * P], KS[0:STACK, h, k0:k0 + wide],
                                    start=True, stop=not masked)
                    if masked:
                        ins = pe.matmul(s[:, diag:diag + P], ident_b[:, :], mask_q[:, :], start=False, stop=True)
                    ins.then_inc(sem["p_nat"], 1)

            def shift(n):
                pe.wait_ge(sem["v_m"], n("v_m", 1))
                pe.wait_ge(sem["a_heads"], n("a_heads"))
                pe.transpose(E[:, 0:P], mm[:, :, :].rearrange("p a b -> p (a b)"), ident[:, :]) \
                    .then_inc(sem["p_shift"], 1)

            def st_(n, i):
                c, kb = SETS[i]
                if i == 0:
                    pe.wait_ge(sem["d_shift"], n("d_shift"))
                skip = max(0, kb - TPC * c) * P
                first = min(skip, W - 2 * P)
                for h in range(HG):
                    if i or h >= 2:
                        pe.wait_ge(sem["a_exp"], n("a_exp", h - 1))
                    masked = kb >= TPC * c
                    s = S[h % 2]
                    ins = pe.matmul(s[:, first:W], KS[0:SHIFT, h, kb * P:(kb + 1) * P],
                                    QS[0:SHIFT, h, c * W + first:(c + 1) * W], start=True, stop=not masked)
                    if masked:
                        ins = pe.matmul(s[:, skip:skip + P], ident_b[:, :], mask_k[:, :], start=False, stop=True)
                    ins.then_inc(sem["p_st"], 1)

            def pv(n, i):
                c, kb = SETS[i]
                skip = max(0, kb - TPC * c) * P
                if i == 0:
                    pe.wait_ge(sem["d_v"], n("d_v"))
                if kb == 0:
                    pe.wait_ge(sem["a_heads"], n("a_heads"))
                last = kb == TPC * (c + 1) - 1
                ahead = 0 if last else HG
                for what, dst in ((vh, O), (ones, E)):
                    for h in range(HG):
                        if what is vh:
                            pe.wait_ge(sem["a_exp"], n("a_exp", h + 1 - HG - ahead))
                        lhs = vh[:, kb, h * DH:(h + 1) * DH] if what is vh else ones[:, :]
                        ins = pe.matmul(dst[h * DH:(h + 1) * DH, skip:W], lhs, pr[:, (i * HG + h) % 8, skip:W],
                                        start=kb == 0, stop=last)
                ins.then_inc(sem["p_pv"], 1)

            def wo_(n, c):
                if c == 0:
                    pe.wait_ge(sem["g_lo"], n.ready("O"))
                pe.wait_ge(sem["v_heads"], n("v_heads"))
                for i in range(TPC):
                    pe.wait_ge(sem["v_dfree"], n("v_dfree", i - 1))
                    rows = slice(i * P, (i + 1) * P)
                    three(Dk[n.dk()][:, :], [((ah[:, rows], al[:, rows]), (woh[:, :], wol[:, :]))]) \
                        .then_inc(sem["p_wo"], 1)

            def gate_up(n, j, blk, fc, wh, wl, dst, kind, free, done):
                if blk == 0 and fc == 0:
                    pe.wait_ge(sem["g_lo"], n.ready(kind))
                pe.wait_ge(sem[free], n(free))
                cols = slice(blk * W, (blk + 1) * W)
                three(dst[:, :], [((wh[:, fc, c, :], wl[:, fc, c, :]), (xh[:, c, cols], xl[:, c, cols]))
                                  for c in range(KC)]).then_inc(sem[done], 1)

            def gate(n, j, blk, fc, nfc):
                gate_up(n, j, blk, fc, wgh, wgl, G, "G", "v_gate", "p_gate")

            def up(n, j, blk, fc, nfc):
                gate_up(n, j, blk, fc, wuh, wul, U, "U", "v_h", "p_up")

            def down(n, j, blk, half, nfc):
                if blk == 0 and half == 0:
                    pe.wait_ge(sem["g_lo"], n.ready("D"))
                pe.wait_ge(sem["g_hl"], n("g_hl"))
                for i in range(TPC // 2):
                    pe.wait_ge(sem["v_dfree"], n("v_dfree", i - 1))
                    r0 = (half * (TPC // 2) + i) * P
                    three(Dk[n.dk()][:, :], [((hh[:, fc, r0:r0 + P], hl[:, fc, r0:r0 + P]),
                                               (wdh[:, fc, :], wdl[:, fc, :])) for fc in range(nfc)]) \
                        .then_inc(sem["p_down"], 1)

            walk(pe, dict(norm=norm, values=values, proj=proj, nat=nat, shift=shift, st=st_, pv=pv, wo=wo_,
                          gate=gate, up=up, down=down))


def chunks(w):
    return w.reshape(-1, P, KC, P).transpose(0, 3, 2, 1)


def pairs_apart(w):
    return w.reshape(H, 2, DH // 2, D).transpose(0, 2, 1, 3).reshape(D, D)


def kernel(**inputs):
    import numpy as np
    import concourse.bacc as bacc
    from concourse.bass_utils import run_bass_kernel_spmd as run

    a = {k: np.asarray(v) for k, v in inputs.items()}
    qk = [(a["L0_attn_Wq"], a["L0_attn_Wk"]), (pairs_apart(a["L1_attn_Wq"]), pairs_apart(a["L1_attn_Wk"]))]
    wqk = np.concatenate([np.stack([chunks(q), chunks(k)], axis=2) for q, k in qk]).reshape(2 * NG, P, -1)
    wo = np.concatenate([a[f"L{i}_attn_Wo"].T.reshape(NG, P, D) for i in range(2)])
    wv = np.stack([a[f"L{i}_attn_Wv"].T.reshape(KC, P, D).transpose(1, 0, 2).reshape(P, -1) for i in range(2)])
    wgate = np.concatenate([chunks(a["L0_ffn_w_gate"]), chunks(a["L1_ffn_gate_w"])]).reshape(-1, P, D)
    wup = np.concatenate([chunks(a["L0_ffn_w_up"]), chunks(a["L1_ffn_up_w"])]).reshape(-1, P, D)
    wdown = np.concatenate([a["L0_ffn_w_down"].T, a["L1_ffn_down_w"].T]).reshape(-1, P, D)
    wqk, wo = (np.concatenate([w, w[:2]]) for w in (wqk, wo))
    wgate, wup, wdown = (np.concatenate([w, w[:4]]) for w in (wgate, wup, wdown))
    scales = np.stack([a[f"L1_ffn_{g}_s"].reshape(-1, P).T for g in ("gate", "up")], axis=2)
    down_s = np.repeat(a["L1_ffn_down_s"].reshape(1, D), P, axis=0)
    half = np.arange(DH // 2, dtype=np.float32)
    theta = [np.float32(10000.0) ** (np.float32(-2.0) * half / np.float32(DH)),
             np.float32(1.0) / np.float32(10000.0) ** (half / np.float32(DH // 2))]
    rope = np.zeros((2, P, 2, T), np.float32)
    for i in range(2):
        angle = np.arange(T, dtype=np.float32)[None, :] * theta[i][:, None]
        for p in range(P):
            k = p % DH
            rope[i, p, 0] = np.cos(angle[k // 2])
            rope[i, p, 1] = np.sin(angle[k // 2]) if k % 2 else -np.sin(angle[k // 2])

    arrays = {"x": a["L0_attn_X"], "wqk": wqk, "wo": wo, "wv": wv, "wgate": wgate, "wup": wup, "wdown": wdown,
              "rope": rope, "scales": scales, "down_s": down_s}
    arrays = {f"in_{k}_dram": np.ascontiguousarray(v) for k, v in arrays.items()}
    nc = bacc.Bacc("TRN2", target_bir_lowering=False, num_devices=1)
    nc.disable_value_cache = True
    args = [nc.dram_tensor(k, v.shape, mybir.dt.from_np(v.dtype), kind="ExternalInput").ap()
            for k, v in arrays.items()]
    args.append(nc.dram_tensor("out_dram", (B, T, D), F32, kind="ExternalOutput").ap())
    two_layers(nc, *args)
    return run(nc, [arrays], core_ids=[0]).results[0]["out_dram"]
```

```python
from contextlib import ExitStack

import concourse.bass as bass
from concourse import mybir

P = 128
B, T, D = 2, 1024, 512
H, DH = 16, 32
HG = P // DH
NG = H // HG
KC = D // P
RT = T // P
W = 512
NC = T // W
TPC = W // P
F0, F1 = 2048, 1408
CH = (F0 // P, F1 // P)
PAIRS = (2, 1)
EPS = 1e-5
SCALE = float(DH) ** -0.5
MASKED = -1e38
STACK = 3 * DH
SHIFT = STACK + 2

F32, F32R, BF16 = mybir.dt.float32, mybir.dt.float32r, mybir.dt.bfloat16
ALU = mybir.AluOpType
ACT = mybir.ActivationFunctionType
AX = mybir.AxisListType



NAT = [(qb, part, (min(qb + 1, TPC) if part == 0 else qb + 1 - TPC) * P)
       for qb in range(RT) for part in range(1 + (qb >= TPC))]
SETS = [(c, kb) for c in range(NC) for kb in range(TPC * (c + 1))]


GU_PARTS = 3


def mlp(layer, sizes):
    out, downs = [], []
    for j, nfc in enumerate(sizes):
        for blk in range(NC):
            for fc in range(nfc):
                last = blk == NC - 1 and fc == nfc - 1
                out += [[("part", "gate", j, blk, fc, k)] for k in range(GU_PARTS - 1)]
                out.append([("gate", j, blk, fc, nfc)] + [("w", "G")] * last)
                out, downs = out + downs, []
                out += [[("part", "up", j, blk, fc, k)] for k in range(GU_PARTS - 1)]
                out.append([("up", j, blk, fc, nfc), ("gated", j, blk, fc, nfc)] + [("w", "U")] * last)
            add = ("add_down", "add_scaled")[layer]
            for i in range(TPC):
                downs.append([("down", j, blk, i, nfc), (add, j, blk, i, nfc)])
            if blk == NC - 1:
                downs[-1].append(("w", "D"))
    return out + downs


def natural():
    return [[("nat", h, u)] for h in range(HG) for u in range(len(NAT))]


def weighted():
    st = [[[("st", 0, h) for h in range(HG)]]]
    for i in range(1, len(SETS) + 1):
        scores = [("st", i, h) for h in range(HG)] if i < len(SETS) else []
        now = [scores[:2] + [("pv", i - 1)], scores[2:] + [("sums", i - 1)]]
        c, kb = SETS[i - 1]
        if kb == TPC * (c + 1) - 1:
            now[-1].append(("heads", c))
        st.append(now)
    return st


def projections():
    proj = [[("proj", t)] for t in range(2 * NC)]
    proj[0].insert(0, ("v_slice", 1))
    proj[-1].append(("w", "A"))
    return proj


def output(c):
    out = [[("wo", c, i), ("add_wo", c, i)] for i in range(TPC)]
    if c == NC - 1:
        out[-1].append(("w", "O"))
    return out


def norms(layer, block):
    return [("norm", layer, rt) for rt in range(block * TPC, (block + 1) * TPC)]


FILL = {"turn0": (6, 28, 4, 8), "turn1": (5, 13, 2, 4), "tail0": (6, 28, 4, 10), "tail1": (6, 36, 4, 10)}
SINGLES = {"turn0": (2, 2), "turn1": (2,), "tail0": (2, 2), "tail1": (2, 2, 1)}


def turn(layer, tail):
    name = ("turn", "tail")[tail] + str(layer)
    pieces = mlp(layer, SINGLES[name])
    a, b, c, d = FILL[name]
    e = len(pieces) - a - b - c - d
    take = iter(pieces)

    def some(k):
        return [next(take) for _ in range(k)]
    out = ([[("v_load", 1)]] if tail and layer == 0 else []) + some(a) + merged(natural(), some(b)) + [[("shift",)]] + some(c)
    st = weighted()
    out += [p for s in st[:TPC + 1] for p in s]
    late = [p for s in st[TPC + 1:] for p in s]
    recip = [[("recip", 0, 0)], [("recip", 0, 1), ("scaled", 0)]]
    late = late[:1] + recip[:1] + late[1:2] + recip[1:] + late[2:6] + output(0) + late[6:]
    out += some(2) + merged(late, some(e - 2))
    if not tail:
        p = projections()
        out += p[:1] + [[("recip", 1, 0)]] + p[1:2] + [[("recip", 1, 1)]] + p[2:3] + [[("scaled", 1)]] + p[3:]
        out += some(d)[:] + output(1)
        return [s for piece in out for s in piece]
    if layer == 0:
        out += [[("v_weights", 1)]]
    chain = [[("recip", 1, 0)], [("recip", 1, 1)], [("scaled", 1)]]
    rest = some(d)
    if layer == 0:
        chain += [[("stats", 1, 0)]]
        out += merged(chain, rest[:4])
        rest = rest[4:]
        n0 = [[x] for x in norms(1, 0)]
        out += merged(output(1) + n0, rest)
    else:
        out += merged(chain, rest[:6]) + [[("store", 0)]] + merged(output(1), rest[6:]) + [[("store", 1)]]
    return [s for piece in out for s in piece]


def merged(a, b):
    out, k = [], 0
    for i, piece in enumerate(a):
        out.append(piece)
        while k < len(b) and (k + 1) * len(a) <= (i + 1) * len(b):
            out.append(b[k])
            k += 1
    return out + b[k:]


def opening(layer):
    out = [("v_load", 0), ("stats", 0, 0), ("v_weights", 0)] + norms(0, 0) if layer == 0 else []
    proj = [("proj", t) for t in range(2 * NC)]
    later = norms(layer, 1)
    out += [("stats", layer, 1), proj[0]]
    for k in range(TPC):
        out += [later[k], ("values", k)]
    out += [proj[1], ("values", 4), proj[2], ("values", 5), ("values", 6), ("values", 7), proj[3]]
    return out + [("w", "A"), ("v_slice", 0)]


ADDS = {
    "v_load": {"d_wv": 16},
    "v_weights": {"d_rope": 16, "v_wv": 1, "g_wv": 1},
    "stats": {"v_chain": 2 * TPC + 5, "v_var": 1, "a_std": 1},
    "norm": {"v_xn": 1, "p_xt": 1, "a_xh": 1, "v_dfree": 1},
    "values": {"p_v": 1, "a_val": 1},
    "v_slice": {"d_v": 16},
    "proj": {"p_proj": 1, "v_pfree": 1, "v_chain": 2, "v_rope": 1, "a_rh": 1, "g_rl": 1},
    "nat": {"p_nat": 1, "v_max": 1},
    "shift": {"v_chain": 2, "v_m": 1, "p_shift": 1, "v_shift": 1, "d_shift": 32},
    "st": {"p_st": 1, "a_exp": 1},
    "pv": {},
    "sums": {"p_pv": 1},
    "heads": {"a_heads": 1},
    "recip": {"v_recip": 1},
    "scaled": {"v_heads": 1, "a_ah": 1, "g_al": 1},
    "wo": {"p_wo": 1},
    "add_wo": {"v_dfree": 1},
    "part": {},
    "gate": {"p_gate": 1, "a_tanh": 1},
    "up": {"p_up": 1},
    "gated": {"v_gate": 1, "v_h": 1, "a_hh": 1, "g_hl": 1},
    "down": {"p_down": 1},
    "add_down": {"v_dfree": 1},
    "add_scaled": {"v_scaled": 1, "v_dfree": 1},
    "w": {"v_hi": 1, "g_lo": 1},
    "store": {},
}
STACKS = 3 * 16

SLOTS = {"open0": "A0", "turn0": "G1 U0 D1 A0 G1 U0 D1 O0", "tail0": "G1 U0 D1 G0 U1 O0 D1",
         "open1": "A0", "turn1": "G1 U0 A1 D0 O1", "tail1": "G1 U0 D1 G0 U1 D0 G1 U0 O1 D0"}
SPLITS_OPEN = [("A", 0), ("O", 1), ("G", 0), ("U", 1), ("D", 0)]

SEMS = sorted({x for a in ADDS.values() for x in a} | {"raw0", "raw1", "d_x0", "d_x1", "d_out"} | {f"d_stack{h}" for h in range(HG)})
CREDIT = {s: 0 if s[0] == "d" or s[:3] == "raw" else 1 for s in SEMS}
CREDIT.update(v_dfree=2, g_hl=2, d_out=16)


class Count:

    def __init__(self):
        self.n = dict(CREDIT)
        self.n["v_hi"] += len(SPLITS_OPEN)
        self.n["g_lo"] += len(SPLITS_OPEN)
        for _, slot in SPLITS_OPEN:
            self.n[f"raw{slot}"] += 16
        self.loops = []
        self.bases = {}
        self.split = 0
        self.d = 0

    def dk(self):
        self.d += 1
        return (self.d - 1) % 2

    def ready(self, kind):
        return self.base("g_lo") + self.w_ready[kind]

    def __call__(self, sem, k=0):
        return self.base(sem) + (self.n[sem] + k)

    def base(self, sem):
        if sem not in self.bases:
            v = 0
            for i, per in self.loops:
                v = i * per[sem] + v
            self.bases[sem] = self.eng.snap(v)
        return self.bases[sem]

    def did(self, step, region):
        for sem, k in ADDS[step[0]].items():
            self.n[sem] += k
        if step[0] == "proj" and step[1] % NC == NC - 1:
            for h in range(HG):
                self.n[f"d_stack{h}"] += STACKS
        if step[0] == "w":
            self.n[f"raw{PLAN[region][self.split][0]}"] += 16
            self.split += 1
        if step[:2] == ("stats", 0):
            self.n[f"d_x{step[2]}"] += 16
        if step[0] == "store":
            self.n["d_out"] += 16


def total(parts):
    c = Count()
    before = dict(c.n)
    for region, steps, times in parts:
        for _ in range(times):
            c.split = 0
            for s in steps:
                c.did(s, region)
    return {k: c.n[k] - before[k] for k in c.n}


REGIONS = []
for _l in (0, 1):
    REGIONS += [(f"open{_l}", opening(_l), 1), (f"turn{_l}", turn(_l, False), NG - 1), (f"tail{_l}", turn(_l, True), 1)]
LAYER = {region: int(region[-1]) for region, _, _ in REGIONS}
MLP_STEP = {"turn0": 2 * PAIRS[0], "turn1": 2 * PAIRS[1]}


def plan_loads():
    seq = []
    at = {k: 0 for k in "AOGUD"}
    for b in range(2):
        size = {k: [w_ for l in (0, 1) for w_ in SIZES_OF[l]] for k in "GUD"}
        for region, steps, times in REGIONS:
            kinds = [s[1] for s in steps if s[0] == "w"]
            slots = SLOTS[region].split()
            assert kinds == [x[0] for x in slots], (region, kinds)
            for g in range(times):
                for k, x in enumerate(slots):
                    at[x[0]] += size[x[0]].pop(0) if x[0] in size else 1
                    seq.append((region, g, k, x[0], int(x[1]), at[x[0]]))
    plan = {}
    for i, (region, g, k, kind, slot, _) in enumerate(seq[:len(seq) // 2]):
        nxt = next(x for x in seq[i + 1:] if x[4] == slot)
        step = 1 if nxt[3] in "AO" else MLP_STEP.get(region, 0)
        entry = (slot, nxt[3], nxt[5] - g * step)
        row = plan.setdefault(region, [])
        if g == 0:
            row.append(entry)
        assert row[k] == entry, (region, g, k, row[k], entry)
    return plan


SIZES_OF = tuple(SINGLES[f"turn{_l}"] * (NG - 1) + SINGLES[f"tail{_l}"] for _l in (0, 1))
PLAN = plan_loads()


def last_splits(region):
    names = [r for r, _, _ in REGIONS]
    i = names.index(region)
    ways = [[x for r in names[:i] for x in SLOTS[r].split()]]
    if i == 0:
        ways = [[x for r in names for x in SLOTS[r].split()]]
    if REGIONS[i][2] > 1:
        ways.append(ways[0] + SLOTS[region].split())
    ways = [[k + str(s_) for k, s_ in SPLITS_OPEN] + w_ for w_ in ways]
    if i == 0:
        ways.append([k + str(s_) for k, s_ in SPLITS_OPEN])
    return {k: min([x[0] for x in reversed(w_)].index(k) for w_ in ways) for k in "AOGUD"}
PER_BATCH = total(REGIONS)


def two_layers(nc, x, wqk, wo, wv, wgate, wup, wdown, rope, scales, down_s, out):
    ctx = ExitStack()
    with ctx:
        def sb(name, shape, dt=F32):
            return ctx.enter_context(nc.sbuf_tensor(name, shape, dt))

        def bank(name):
            return ctx.enter_context(nc.psum_tensor(name, [P, W], F32))

        sem = {s: ctx.enter_context(nc.semaphore(s)) for s in SEMS}
        s_const = ctx.enter_context(nc.semaphore("s_const"))
        d_const = ctx.enter_context(nc.semaphore("d_const"))
        s_vconst = ctx.enter_context(nc.semaphore("s_vconst"))

        xres = sb("xres", [P, RT, D])
        xh, xl = sb("xh", [P, KC, T], F32R), sb("xl", [P, KC, T], F32R)
        val = sb("val", [P, RT, D])
        vh = sb("vh", [P, RT, P])
        raw = sb("raw", [P, 2, 2 * W])
        wqkh, wqkl = sb("wqkh", [P, 2, KC, P], F32R), sb("wqkl", [P, 2, KC, P], F32R)
        woh, wol = sb("woh", [P, D], F32R), sb("wol", [P, D], F32R)
        wgh, wgl = sb("wgh", [P, 2, KC, P], F32R), sb("wgl", [P, 2, KC, P], F32R)
        wuh, wul = sb("wuh", [P, 2, KC, P], F32R), sb("wul", [P, 2, KC, P], F32R)
        wdh, wdl = sb("wdh", [P, 2, D], F32R), sb("wdl", [P, 2, D], F32R)
        QS, KS = sb("QS", [P, HG, T], F32R), sb("KS", [P, HG, T], F32R)
        wvh = QS[:, 0:2, :].rearrange("p a (b n) -> p (a b) n", n=D)
        wvl = QS[:, 2:4, :].rearrange("p a (b n) -> p (a b) n", n=D)
        swapped = sb("swapped", [P, W])
        trig = sb("trig", [P, 2, T])
        wv_raw = trig[:, :, :].rearrange("p a (b n) -> p (a b) n", n=D)
        pr = sb("pr", [P, 8, W])
        flat_h = [pr[:, 2 * NC * k:2 * NC * k + NC, :].rearrange("p c n -> p (c n)") for k in range(2)]
        flat_l = [pr[:, 2 * NC * k + NC:2 * NC * (k + 1), :].rearrange("p c n -> p (c n)") for k in range(2)]
        xn = sb("xn", [P, 2, D])
        heads, denom = sb("heads", [P, W]), sb("denom", [P, W])
        ah, al = sb("ah", [P, W], F32R), sb("al", [P, W], F32R)
        tt = sb("tt", [P, 2, W])
        hh, hl = sb("hh", [P, 2, W], F32R), sb("hl", [P, 2, W], F32R)
        ds = sb("ds", [P, D])
        ident = sb("ident", [P, P])
        ident_b = sb("ident_b", [P, P], BF16)
        mask_q, mask_k = sb("mask_q", [P, P], BF16), sb("mask_k", [P, P], BF16)
        ones = sb("ones", [P, DH])
        mp = sb("mp", [P, HG * RT, 2])
        mx = sb("mx", [P, HG * RT])
        mm = sb("mm", [P, P // (HG * RT), HG * RT])
        mt = sb("mt", [2 * HG * RT, P], F32R)
        stat6 = sb("stat6", [P, RT, 6])
        mv = sb("mv", [P, RT, 2])
        st = sb("st", [P, NC, 6, TPC])
        sc = sb("sc", [P, CH[1], 2])
        half_gs, both_s = sb("half_gs", [P, CH[1]]), sb("both_s", [P, CH[1]])

        S = [bank("S0"), bank("S1")]
        G, U = bank("G"), bank("U")
        Dk = [bank("D0"), bank("D1")]
        O, E = bank("O"), bank("E")
        NB = S + [O, E]

        SPLIT_TO = {"A": (wqkh, wqkl), "O": (woh, wol), "G": (wgh, wgl), "U": (wuh, wul), "D": (wdh, wdl)}
        SIZE = {"A": 2 * W, "O": W, "G": 2 * W, "U": 2 * W, "D": 2 * W}
        FREED_BY = {"A": "p_proj", "O": "p_wo", "G": "p_gate", "U": "p_up", "D": "p_down"}

        def flat(t):
            return t[:, :] if len(t.shape) == 2 else t[:, :, :].rearrange("p a b -> p (a b)") \
                if len(t.shape) == 3 else t[:, :, :, :].rearrange("p a b c -> p (a b c)")

        def load(sp, kind, at, slot):
            dst = raw[:, slot, 0:SIZE[kind]]
            if kind in "AO":
                src = (wqk if kind == "A" else wo)[bass.ds(at, 1), :, :].rearrange("a p n -> p (a n)")
            else:
                src = {"G": wgate, "U": wup, "D": wdown}[kind][bass.ds(at, 2), :, :].rearrange("a p n -> p a n")
                dst = dst.rearrange("p (a n) -> p a n", a=2)
            sp.dma_start(dst, src).then_inc(sem[f"raw{slot}"], 16)

        def walk(eng, part):
            with eng.Fori(0, B) as b:
                n = Count()
                n.eng, n.b = eng, b
                n.loops.append((b, PER_BATCH))
                n.part = part
                for region, steps, times in REGIONS:
                    n.region, n.layer = region, LAYER[region]
                    n.split, n.d, n.turns = 0, 0, NG - 1 if region[:4] == "tail" else 0
                    n.turns_w = 0
                    n.w_ready = {k: n.n["g_lo"] - d for k, d in last_splits(region).items()}
                    n.bases = {}
                    if times == 1:
                        walk_steps(n, steps)
                        continue
                    start = dict(n.n)
                    with eng.Fori(0, times) as g:
                        per = total([(region, steps, 1)])
                        n.loops.append((g, per))
                        n.bases = {}
                        n.turns = n.turns_w = g
                        walk_steps(n, steps)
                        n.loops.pop()
                    for k in start:
                        n.n[k] = start[k] + times * (n.n[k] - start[k])

        def walk_steps(n, steps):
            for s in steps:
                if s[0] in n.part:
                    n.part[s[0]](n, *s[1:])
                n.did(s, n.region)
                if s[0] == "w":
                    n.w_ready[s[1]] = n.n["g_lo"]

        def chunk(n, j, fc):
            at = n.turns * (2 * PAIRS[1]) + (2 * j + fc)
            return bass.ds(at, 1)

        block = ctx.enter_context(nc.Block())

        @block.sync
        def _(sp):
            for s in SEMS:
                if CREDIT[s]:
                    sp.sem_inc(sem[s], CREDIT[s])
            sp.dma_start(sc[:, :, :], scales).then_inc(d_const, 16)
            sp.dma_start(ds[:, :], down_s).then_inc(d_const, 16)
            for i, (kind, slot) in enumerate(SPLITS_OPEN):
                if i >= 2:
                    sp.wait_ge(sem["g_lo"], CREDIT["g_lo"] + i - 1)
                load(sp, kind, 0, slot)
            sp.wait_ge(sem["g_lo"], CREDIT["g_lo"] + 4)
            load(sp, "G", 2, 1)
            sp.wait_ge(sem["g_lo"], CREDIT["g_lo"] + 5)
            load(sp, "A", 1, 0)

            def v_load(n, layer):
                sp.wait_ge(sem["g_rl"], n("g_rl"))
                sp.dma_start(wv_raw, wv[layer].rearrange("p (c n) -> p c n", c=KC)).then_inc(sem["d_wv"], 16)

            def v_weights(n, layer):
                sp.wait_ge(sem["g_wv"], n("g_wv", 1))
                sp.dma_start(trig[:, :, :], rope[layer]).then_inc(sem["d_rope"], 16)

            def rows(dram, n, c):
                return dram[bass.ds(n.b, 1), c * W:(c + 1) * W, :].rearrange("a (t p) d -> p (a t) d", p=P)

            def stats(n, layer, c):
                if layer == 0:
                    sp.wait_ge(sem["d_out"], n("d_out"))
                    sp.dma_start(xres[:, c * TPC:(c + 1) * TPC, :], rows(x, n, c)).then_inc(sem[f"d_x{c}"], 16)

            def v_slice(n, ahead):
                sp.wait_ge(sem["p_pv"], n("p_pv"))
                sp.wait_ge(sem["a_val"], n("a_val"))
                sp.dma_start(vh[:, :, :], val[:, :, bass.ds((n.turns + ahead) * P, P)]).then_inc(sem["d_v"], 16)

            def proj(n, t):
                if t % NC < NC - 1:
                    return
                qk = t // NC
                flats = ((flat_h, flat_h, flat_l), (flat_h, flat_l, flat_h))[qk]
                sp.wait_ge(sem["g_rl"], n("g_rl", 1))
                for h in range(HG):
                    for r, src in enumerate(flats):
                        sp.dma_start((KS, QS)[qk][r * DH:(r + 1) * DH, h, :].bitcast(F32),
                                     src[qk][h * DH:(h + 1) * DH, :]).then_inc(sem[f"d_stack{h}"], 16)

            def shift(n):
                sp.wait_ge(sem["v_shift"], n("v_shift", 1))
                for k in range(2):
                    sp.dma_start(QS[STACK + k:STACK + k + 1, :, :].rearrange("o h (q n) -> o (h q) n", n=P).bitcast(F32),
                                 mt[k * HG * RT:(k + 1) * HG * RT, :].bitcast(F32)).then_inc(sem["d_shift"], 16)

            def w(n, kind):
                slot, nxt, at = PLAN[n.region][n.split]
                sp.wait_ge(sem["g_lo"], n("g_lo", 1))
                load(sp, nxt, n.turns_w * (1 if nxt in "AO" else MLP_STEP.get(n.region, 0)) + at, slot)

            def store(n, c):
                sp.wait_ge(sem["v_dfree"], n("v_dfree"))
                sp.dma_start(rows(out, n, c), xres[:, c * TPC:(c + 1) * TPC, :]).then_inc(sem["d_out"], 16)

            walk(sp, dict(v_load=v_load, v_weights=v_weights, stats=stats, v_slice=v_slice, proj=proj, shift=shift, w=w, store=store))
            sp.wait_ge(sem["d_out"], CREDIT["d_out"] + 16 * NC * B)
            for k in range(2):
                sp.wait_ge(sem[f"raw{k}"], 16 * sum(s == k for _, s in SPLITS_OPEN) + B * PER_BATCH[f"raw{k}"] + 16)

        @block.scalar
        def _(act):
            def stats(n, layer, c):
                act.wait_ge(sem["v_var"], n("v_var", 1))
                act.activation(st[:, c, 1, :], st[:, c, 0, :], ACT.Sqrt).then_inc(sem["a_std"], 1)

            def norm(n, layer, rt):
                act.wait_ge(sem["p_xt"], n("p_xt", 1))
                act.copy(xh[:, :, rt * P:(rt + 1) * P], Dk[n.dk()][:, :].rearrange("p (c n) -> p c n", c=KC)) \
                    .then_inc(sem["a_xh"], 1)

            def values(n, rt):
                act.wait_ge(sem["p_v"], n("p_v", 1))
                act.copy(val[:, rt, :], (O, E)[rt % 2][:, :]).then_inc(sem["a_val"], 1)

            def other_bank(n, *_):
                n.dk()

            def proj(n, t):
                act.wait_ge(sem["v_rope"], n("v_rope", 1))
                cols = slice((t % NC) * W, (t % NC + 1) * W)
                act.copy(flat_h[t // NC][:, cols].bitcast(F32R), flat_l[t // NC][:, cols]).then_inc(sem["a_rh"], 1)

            def st_(n, i, h):
                c, kb = SETS[i]
                skip = max(0, kb - TPC * c) * P
                act.wait_ge(sem["p_st"], n("p_st", 1))
                act.wait_ge(sem["p_pv"], n("p_pv"))
                act.activation(pr[:, (i * HG + h) % 8, skip:W], S[h % 2][:, skip:W], ACT.Exp, scale=SCALE) \
                    .then_inc(sem["a_exp"], 1)

            def heads_(n, c):
                act.wait_ge(sem["p_pv"], n("p_pv"))
                act.wait_ge(sem["g_al"], n("g_al"))
                act.copy(heads[:, :], O[:, :])
                act.copy(denom[:, :], E[:, :]).then_inc(sem["a_heads"], 1)

            def scaled(n, c):
                act.wait_ge(sem["v_heads"], n("v_heads", 1))
                act.wait_ge(sem["p_wo"], n("p_wo"))
                act.copy(ah[:, :], heads[:, :]).then_inc(sem["a_ah"], 1)

            def gate(n, j, blk, fc, nfc):
                act.wait_ge(sem["p_gate"], n("p_gate", 1))
                act.wait_ge(sem["g_hl"], n("g_hl", -1))
                par = (blk * nfc + fc) % 2
                act.activation(tt[:, par, :], G[:, :], ACT.Tanh,
                               scale=half_gs[:, chunk(n, j, fc)] if n.layer else 0.5).then_inc(sem["a_tanh"], 1)

            def gated(n, j, blk, fc, nfc):
                act.wait_ge(sem["v_h"], n("v_h", 1))
                act.wait_ge(sem["p_down"], n("p_down"))
                act.copy(hh[:, fc, :], tt[:, (blk * nfc + fc) % 2, :]).then_inc(sem["a_hh"], 1)

            act.wait_ge(s_vconst, 2)
            walk(act, dict(stats=stats, norm=norm, values=values, proj=proj, st=st_, heads=heads_, gate=gate,
                           gated=gated, scaled=scaled, down=other_bank, wo=other_bank))

        @block.gpsimd
        def _(pool):
            pool.memset(ident[:, :], 1.0).then_inc(s_const, 1)
            pool.memset(ident_b[:, :], 1.0).then_inc(s_const, 1)
            pool.memset(mask_q[:, :], 0.0).then_inc(s_const, 1)
            pool.memset(mask_k[:, :], 0.0).then_inc(s_const, 1)
            pool.wait_ge(s_const, 4)
            for t in (ident, ident_b):
                pool.affine_select(out=t[:, :], in_=t[:, :], pattern=[[1, P]], compare_op=ALU.is_equal, fill=0.0,
                                   base=0, channel_multiplier=-1).then_inc(s_const, 1)
            pool.affine_select(out=mask_q[:, :], in_=mask_q[:, :], pattern=[[-1, P]], compare_op=ALU.is_ge,
                               fill=MASKED, base=0, channel_multiplier=1).then_inc(s_const, 1)
            pool.affine_select(out=mask_k[:, :], in_=mask_k[:, :], pattern=[[1, P]], compare_op=ALU.is_ge,
                               fill=MASKED, base=0, channel_multiplier=-1).then_inc(s_const, 1)

            def low(kind, slot):
                hi, lo = SPLIT_TO[kind]
                return pool.tensor_tensor(flat(lo), raw[:, slot, 0:SIZE[kind]], flat(hi).bitcast(F32), ALU.subtract)

            for i, (kind, slot) in enumerate(SPLITS_OPEN):
                pool.wait_ge(sem["v_hi"], CREDIT["v_hi"] + i + 1)
                low(kind, slot).then_inc(sem["g_lo"], 1)

            def v_weights(n, layer):
                pool.wait_ge(sem["v_wv"], n("v_wv", 1))
                pool.tensor_tensor(wvl, wv_raw, wvh.bitcast(F32), ALU.subtract).then_inc(sem["g_wv"], 1)

            def w(n, kind):
                pool.wait_ge(sem["v_hi"], n("v_hi", 1))
                low(kind, PLAN[n.region][n.split][0]).then_inc(sem["g_lo"], 1)

            def gated(n, j, blk, fc, nfc):
                pool.wait_ge(sem["a_hh"], n("a_hh", 1))
                pool.tensor_tensor(hl[:, fc, :], tt[:, (blk * nfc + fc) % 2, :], hh[:, fc, :].bitcast(F32), ALU.subtract) \
                    .then_inc(sem["g_hl"], 1)

            def proj(n, t):
                pool.wait_ge(sem["a_rh"], n("a_rh", 1))
                cols = slice((t % NC) * W, (t % NC + 1) * W)
                lo = flat_l[t // NC][:, cols]
                pool.tensor_tensor(lo.bitcast(F32R), lo, flat_h[t // NC][:, cols], ALU.subtract).then_inc(sem["g_rl"], 1)

            def scaled(n, c):
                pool.wait_ge(sem["a_ah"], n("a_ah", 1))
                pool.tensor_tensor(al[:, :], heads[:, :], ah[:, :].bitcast(F32), ALU.subtract).then_inc(sem["g_al"], 1)

            walk(pool, dict(v_weights=v_weights, w=w, gated=gated, proj=proj, scaled=scaled))

        @block.vector
        def _(dve):
            def high(kind, slot):
                return dve.tensor_copy(flat(SPLIT_TO[kind][0]), raw[:, slot, 0:SIZE[kind]])

            dve.memset(ones[:, :], 1.0)
            dve.memset(mp[:, :, :], -3e38)
            dve.memset(mm[:, :, :], 0.0)
            dve.memset(KS[STACK:P, :, :].bitcast(F32), 1.0)
            dve.wait_ge(d_const, 32)
            dve.tensor_scalar(half_gs[:, :], sc[:, :, 0], 0.5, None, ALU.mult).then_inc(s_vconst, 1)
            dve.wait_ge(s_vconst, 1)
            dve.tensor_tensor(both_s[:, :], half_gs[:, :], sc[:, :, 1], ALU.mult).then_inc(s_vconst, 1)
            dve.wait_ge(s_vconst, 2)
            opened = {0: 0, 1: 0}
            for kind, slot in SPLITS_OPEN:
                opened[slot] += 16
                dve.wait_ge(sem[f"raw{slot}"], opened[slot])
                high(kind, slot).then_inc(sem["v_hi"], 1)

            def linker(n):
                k = [0]

                def link(ins, ordered=True):
                    k[0] += 1
                    ins.then_inc(sem["v_chain"], 1)
                    if ordered:
                        dve.wait_ge(sem["v_chain"], n("v_chain", k[0]))
                return link

            def v_weights(n, layer):
                dve.wait_ge(sem["d_wv"], n("d_wv"))
                dve.wait_ge(sem["p_st"], n("p_st"))
                dve.tensor_copy(wvh, wv_raw).then_inc(sem["v_wv"], 1)

            def stats(n, layer, c):
                link = linker(n)
                if layer == 0:
                    dve.wait_ge(sem[f"d_x{c}"], n(f"d_x{c}", 16))
                else:
                    dve.wait_ge(sem["v_dfree"], n("v_dfree"))
                tiles = range(c * TPC, (c + 1) * TPC)
                t = st[:, c]
                for rt in tiles:
                    link(dve.bn_stats(stat6[:, rt, :], xres[:, rt, :]), rt == tiles[-1])
                dve.memset(t[:, 2, :], 0.0)
                for rt in tiles:
                    link(dve.bn_aggr(mv[:, rt, :], stat6[:, rt, :]), rt == tiles[-1])
                dve.tensor_scalar(t[:, 0, :], mv[:, tiles[0]:tiles[-1] + 1, 1], EPS, None, ALU.add).then_inc(sem["v_var"], 1)
                dve.wait_ge(sem["v_var"], n("v_var", 1))
                dve.wait_ge(sem["a_std"], n("a_std", 1))
                link(dve.reciprocal(t[:, 2, :], t[:, 1, :]))
                link(dve.tensor_tensor(t[:, 3, :], t[:, 0, :], t[:, 2, :], ALU.mult))
                link(dve.tensor_tensor(t[:, 4, :], t[:, 3, :], t[:, 1, :], ALU.add))
                link(dve.reciprocal(t[:, 3, :], t[:, 4, :]))
                link(dve.tensor_scalar(t[:, 5, :], t[:, 3, :], 2.0, None, ALU.mult))

            def norm(n, layer, rt):
                dve.wait_ge(sem["p_xt"], n("p_xt", -1 if rt else 0))
                dve.tensor_scalar(xn[:, rt % 2, :], xres[:, rt, :], mv[:, rt, 0:1], st[:, rt // TPC, 5, rt % TPC:rt % TPC + 1],
                                  ALU.subtract, ALU.mult).then_inc(sem["v_xn"], 1)
                dve.wait_ge(sem["a_xh"], n("a_xh", 1))
                dve.tensor_tensor(xl[:, :, rt * P:(rt + 1) * P],
                                  Dk[n.dk()][:, :].rearrange("p (c n) -> p c n", c=KC),
                                  xh[:, :, rt * P:(rt + 1) * P].bitcast(F32), ALU.subtract) \
                    .then_inc(sem["v_dfree"], 1)

            def proj(n, t):
                cols = slice((t % NC) * W, (t % NC + 1) * W)
                turned = flat_l[t // NC][:, cols]
                if t == 0:
                    dve.wait_ge(sem["d_rope"], n("d_rope"))
                dve.wait_ge(sem["p_proj"], n("p_proj", 1))
                dve.wait_ge(sem["v_rope"], n("v_rope"))
                dve.tensor_tensor(turned, S[t % 2][:, :], trig[:, 0, cols], ALU.mult).then_inc(sem["v_pfree"], 1)
                dve.stream_shuffle(swapped[:, :], S[t % 2][:, :], [i ^ 1 for i in range(32)]) \
                    .then_inc(sem["v_chain"], 1)
                dve.wait_ge(sem["v_chain"], n("v_chain", 1))
                dve.tensor_tensor(swapped[:, :], swapped[:, :], trig[:, 1, cols], ALU.mult).then_inc(sem["v_chain"], 1)
                dve.wait_ge(sem["v_chain"], n("v_chain", 2))
                dve.wait_ge(sem["v_pfree"], n("v_pfree", 1))
                dve.tensor_tensor(turned, turned, swapped[:, :], ALU.add).then_inc(sem["v_rope"], 1)

            def nat(n, h, u):
                qb, part, w_ = NAT[u]
                dve.wait_ge(sem["p_nat"], n("p_nat", 1))
                dve.tensor_reduce(mp[:, h * RT + qb, part:part + 1], NB[(h * len(NAT) + u) % 4][:, 0:w_], AX.X, ALU.max) \
                    .then_inc(sem["v_max"], 1)

            def shift(n):
                link = linker(n)
                dve.wait_ge(sem["v_max"], n("v_max"))
                link(dve.tensor_reduce(mx[:, :], mp[:, :, :], AX.X, ALU.max))
                link(dve.tensor_scalar(mm[:, 0, :].bitcast(F32R), mx[:, :], -1.0, None, ALU.mult))
                dve.scalar_tensor_tensor(mm[:, 1, :], mx[:, :], -1.0, mm[:, 0, :], ALU.mult, ALU.subtract) \
                    .then_inc(sem["v_m"], 1)
                dve.wait_ge(sem["p_shift"], n("p_shift", 1))
                dve.tensor_copy(mt[:, :], E[0:2 * HG * RT, 0:P]).then_inc(sem["v_shift"], 1)

            def recip(n, c, k):
                dve.wait_ge(sem["a_heads"], n("a_heads"))
                half = slice(k * W // 2, (k + 1) * W // 2)
                dve.reciprocal(denom[:, half], denom[:, half]).then_inc(sem["v_recip"], 1)

            def scaled(n, c):
                dve.wait_ge(sem["v_recip"], n("v_recip"))
                dve.tensor_tensor(heads[:, :], heads[:, :], denom[:, :], ALU.mult).then_inc(sem["v_heads"], 1)

            def add(n, done, rt):
                dve.wait_ge(sem[done], n(done))
                dve.wait_ge(sem["v_dfree"], n("v_dfree"))
                d = Dk[n.dk()]
                if n.layer and done == "p_down":
                    dve.tensor_tensor(d[:, :], d[:, :], ds[:, :], ALU.mult).then_inc(sem["v_scaled"], 1)
                    dve.wait_ge(sem["v_scaled"], n("v_scaled", 1))
                dve.tensor_tensor(xres[:, rt, :], d[:, :], xres[:, rt, :], ALU.add).then_inc(sem["v_dfree"], 1)

            def add_wo(n, c, i):
                add(n, "p_wo", c * TPC + i)

            def add_down(n, j, blk, i, nfc):
                add(n, "p_down", blk * TPC + i)

            def gated(n, j, blk, fc, nfc):
                t = tt[:, (blk * nfc + fc) % 2, :]
                dve.wait_ge(sem["a_tanh"], n("a_tanh"))
                dve.scalar_tensor_tensor(t, t, 1.0, G[:, :], ALU.add, ALU.mult).then_inc(sem["v_gate"], 1)
                dve.wait_ge(sem["v_gate"], n("v_gate", 1))
                dve.wait_ge(sem["p_up"], n("p_up"))
                dve.scalar_tensor_tensor(t, t, both_s[:, chunk(n, j, fc)] if n.layer else 0.5, U[:, :],
                                         ALU.mult, ALU.mult).then_inc(sem["v_h"], 1)

            def w(n, kind):
                slot = PLAN[n.region][n.split][0]
                dve.wait_ge(sem[f"raw{slot}"], n(f"raw{slot}", 16))
                dve.wait_ge(sem[FREED_BY[kind]], n(FREED_BY[kind]))
                high(kind, slot).then_inc(sem["v_hi"], 1)

            walk(dve, dict(v_weights=v_weights, stats=stats, norm=norm, proj=proj, nat=nat, shift=shift,
                           recip=recip, scaled=scaled, add_wo=add_wo, add_down=add_down, add_scaled=add_down, gated=gated, w=w))

        @block.tensor
        def _(pe):
            pe.wait_ge(s_const, 8)
            pe.wait_ge(s_vconst, 2)

            def three(dst, terms, k=0, parts=1):
                seq = [m for (ah_, al_), (bh, bl) in terms for m in ((ah_, bh), (ah_, bl), (al_, bh))]
                size = len(seq) // parts
                for i in range(k * size, (k + 1) * size):
                    a, b_ = seq[i]
                    ins = pe.matmul(dst, a, b_, start=i == 0, stop=i == len(seq) - 1)
                return ins

            def norm(n, layer, rt):
                pe.wait_ge(sem["v_xn"], n("v_xn", 1))
                pe.wait_ge(sem["v_dfree"], n("v_dfree", -1))
                d = Dk[n.dk()]
                for c in range(KC):
                    ins = pe.transpose(d[:, c * P:(c + 1) * P], xn[:, rt % 2, c * P:(c + 1) * P], ident[:, :])
                ins.then_inc(sem["p_xt"], 1)

            def values(n, rt):
                if rt == 0:
                    pe.wait_ge(sem["g_wv"], n("g_wv"))
                pe.wait_ge(sem["v_dfree"], n("v_dfree"))
                if rt < 2:
                    pe.wait_ge(sem["a_heads"], n("a_heads"))
                else:
                    pe.wait_ge(sem["a_val"], n("a_val", -1))
                rows = slice(rt * P, (rt + 1) * P)
                three((O, E)[rt % 2][:, :], [((xh[:, c, rows], xl[:, c, rows]), (wvh[:, c, :], wvl[:, c, :]))
                                             for c in range(KC)]).then_inc(sem["p_v"], 1)

            def proj(n, t):
                if t == 0:
                    pe.wait_ge(sem["g_lo"], n.ready("A"))
                if n.region[:4] == "open":
                    pe.wait_ge(sem["v_dfree"], n("v_dfree"))
                if t < 2:
                    pe.wait_ge(sem["a_exp"], n("a_exp"))
                else:
                    pe.wait_ge(sem["v_rope"], n("v_rope", -1))
                cols = slice((t % NC) * W, (t % NC + 1) * W)
                qk = 1 - t // NC
                three(S[t % 2][:, :], [((wqkh[:, qk, c, :], wqkl[:, qk, c, :]), (xh[:, c, cols], xl[:, c, cols]))
                                       for c in range(KC)]).then_inc(sem["p_proj"], 1)

            def nat(n, h, u):
                if u == 0:
                    pe.wait_ge(sem[f"d_stack{h}"], n(f"d_stack{h}"))
                if h == 0 and u < 4:
                    pe.wait_ge(sem["a_heads"], n("a_heads"))
                    pe.wait_ge(sem["a_val"], n("a_val"))
                else:
                    pe.wait_ge(sem["v_max"], n("v_max", -3))
                qb, part, w_ = NAT[u]
                k0 = part * W
                diag = qb * P - k0
                s = NB[(h * len(NAT) + u) % 4]
                wide = max(w_, 2 * P)
                masked = diag == w_ - P
                ins = pe.matmul(s[:, 0:wide], QS[0:STACK, h, qb * P:(qb + 1) * P], KS[0:STACK, h, k0:k0 + wide],
                                start=True, stop=not masked)
                if masked:
                    ins = pe.matmul(s[:, diag:diag + P], ident_b[:, :], mask_q[:, :], start=False, stop=True)
                ins.then_inc(sem["p_nat"], 1)

            def shift(n):
                pe.wait_ge(sem["v_m"], n("v_m", 1))
                pe.transpose(E[:, 0:P], mm[:, :, :].rearrange("p a b -> p (a b)"), ident[:, :]) \
                    .then_inc(sem["p_shift"], 1)

            def st_(n, i, h):
                c, kb = SETS[i]
                if i == 0 and h == 0:
                    pe.wait_ge(sem["d_shift"], n("d_shift"))
                skip = max(0, kb - TPC * c) * P
                first = min(skip, W - 2 * P)
                if i or h >= 2:
                    pe.wait_ge(sem["a_exp"], n("a_exp", -1))
                masked = kb >= TPC * c
                s = S[h % 2]
                ins = pe.matmul(s[:, first:W], KS[0:SHIFT, h, kb * P:(kb + 1) * P],
                                QS[0:SHIFT, h, c * W + first:(c + 1) * W], start=True, stop=not masked)
                if masked:
                    ins = pe.matmul(s[:, skip:skip + P], ident_b[:, :], mask_k[:, :], start=False, stop=True)
                ins.then_inc(sem["p_st"], 1)

            def pv(n, i):
                c, kb = SETS[i]
                skip = max(0, kb - TPC * c) * P
                if i == 0:
                    pe.wait_ge(sem["d_v"], n("d_v"))
                if kb == 0:
                    pe.wait_ge(sem["a_heads"], n("a_heads"))
                pe.wait_ge(sem["a_exp"], n("a_exp", -2 if i < len(SETS) - 1 else 0))
                for h in range(HG):
                    pe.matmul(O[h * DH:(h + 1) * DH, skip:W], vh[:, kb, h * DH:(h + 1) * DH],
                              pr[:, (i * HG + h) % 8, skip:W], start=kb == 0, stop=kb == TPC * (c + 1) - 1)

            def sums(n, i):
                c, kb = SETS[i]
                skip = max(0, kb - TPC * c) * P
                for h in range(HG):
                    ins = pe.matmul(E[h * DH:(h + 1) * DH, skip:W], ones[:, :], pr[:, (i * HG + h) % 8, skip:W],
                                    start=kb == 0, stop=kb == TPC * (c + 1) - 1)
                ins.then_inc(sem["p_pv"], 1)

            def wo_(n, c, i):
                if c == 0 and i == 0:
                    pe.wait_ge(sem["g_lo"], n.ready("O"))
                if i == 0:
                    pe.wait_ge(sem["g_al"], n("g_al"))
                pe.wait_ge(sem["v_dfree"], n("v_dfree", -1))
                rows = slice(i * P, (i + 1) * P)
                three(Dk[n.dk()][:, :], [((ah[:, rows], al[:, rows]), (woh[:, :], wol[:, :]))]) \
                    .then_inc(sem["p_wo"], 1)

            def gate_up(n, kind, j, blk, fc, k):
                wh, wl, dst, w_kind, free = {"gate": (wgh, wgl, G, "G", "v_gate"), "up": (wuh, wul, U, "U", "v_h")}[kind]
                if k == 0 and blk == 0 and fc == 0:
                    pe.wait_ge(sem["g_lo"], n.ready(w_kind))
                if k == 0:
                    pe.wait_ge(sem[free], n(free))
                cols = slice(blk * W, (blk + 1) * W)
                return three(dst[:, :], [((wh[:, fc, c, :], wl[:, fc, c, :]), (xh[:, c, cols], xl[:, c, cols]))
                                         for c in range(KC)], k, GU_PARTS)

            def gate(n, j, blk, fc, nfc):
                gate_up(n, "gate", j, blk, fc, GU_PARTS - 1).then_inc(sem["p_gate"], 1)

            def up(n, j, blk, fc, nfc):
                gate_up(n, "up", j, blk, fc, GU_PARTS - 1).then_inc(sem["p_up"], 1)

            def down(n, j, blk, i, nfc):
                if blk == 0 and i == 0:
                    pe.wait_ge(sem["g_lo"], n.ready("D"))
                if i == 0:
                    pe.wait_ge(sem["g_hl"], n("g_hl"))
                pe.wait_ge(sem["v_dfree"], n("v_dfree", -1))
                three(Dk[n.dk()][:, :], [((hh[:, fc, i * P:(i + 1) * P], hl[:, fc, i * P:(i + 1) * P]),
                                          (wdh[:, fc, :], wdl[:, fc, :])) for fc in range(nfc)]) \
                    .then_inc(sem["p_down"], 1)

            walk(pe, dict(norm=norm, values=values, proj=proj, nat=nat, shift=shift, st=st_, pv=pv, sums=sums, wo=wo_,
                          gate=gate, up=up, part=gate_up, down=down))


def chunks(w):
    return w.reshape(-1, P, KC, P).transpose(0, 3, 2, 1)


def pairs_apart(w):
    return w.reshape(H, 2, DH // 2, D).transpose(0, 2, 1, 3).reshape(D, D)


def kernel(**inputs):
    import numpy as np
    import concourse.bacc as bacc
    from concourse.bass_utils import run_bass_kernel_spmd as run

    a = {k: np.asarray(v) for k, v in inputs.items()}
    qk = [(a["L0_attn_Wq"], a["L0_attn_Wk"]), (pairs_apart(a["L1_attn_Wq"]), pairs_apart(a["L1_attn_Wk"]))]
    wqk = np.concatenate([np.stack([chunks(q), chunks(k)], axis=2) for q, k in qk]).reshape(2 * NG, P, -1)
    wo = np.concatenate([a[f"L{i}_attn_Wo"].T.reshape(NG, P, D) for i in range(2)])
    wv = np.stack([a[f"L{i}_attn_Wv"].T.reshape(KC, P, D).transpose(1, 0, 2).reshape(P, -1) for i in range(2)])
    wgate = np.concatenate([chunks(a["L0_ffn_w_gate"]), chunks(a["L1_ffn_gate_w"])]).reshape(-1, P, D)
    wup = np.concatenate([chunks(a["L0_ffn_w_up"]), chunks(a["L1_ffn_up_w"])]).reshape(-1, P, D)
    wdown = np.concatenate([a["L0_ffn_w_down"].T, a["L1_ffn_down_w"].T]).reshape(-1, P, D)
    wqk, wo = (np.concatenate([w, w[:2]]) for w in (wqk, wo))
    wgate, wup, wdown = (np.concatenate([w, w[:4]]) for w in (wgate, wup, wdown))
    scales = np.stack([a[f"L1_ffn_{g}_s"].reshape(-1, P).T for g in ("gate", "up")], axis=2)
    down_s = np.repeat(a["L1_ffn_down_s"].reshape(1, D), P, axis=0)
    half = np.arange(DH // 2, dtype=np.float32)
    theta = [np.float32(10000.0) ** (np.float32(-2.0) * half / np.float32(DH)),
             np.float32(1.0) / np.float32(10000.0) ** (half / np.float32(DH // 2))]
    rope = np.zeros((2, P, 2, T), np.float32)
    for i in range(2):
        angle = np.arange(T, dtype=np.float32)[None, :] * theta[i][:, None]
        for p in range(P):
            k = p % DH
            rope[i, p, 0] = np.cos(angle[k // 2])
            rope[i, p, 1] = np.sin(angle[k // 2]) if k % 2 else -np.sin(angle[k // 2])

    arrays = {"x": a["L0_attn_X"], "wqk": wqk, "wo": wo, "wv": wv, "wgate": wgate, "wup": wup, "wdown": wdown,
              "rope": rope, "scales": scales, "down_s": down_s}
    arrays = {f"in_{k}_dram": np.ascontiguousarray(v) for k, v in arrays.items()}
    nc = bacc.Bacc("TRN2", target_bir_lowering=False, num_devices=1)
    nc.disable_value_cache = True
    args = [nc.dram_tensor(k, v.shape, mybir.dt.from_np(v.dtype), kind="ExternalInput").ap()
            for k, v in arrays.items()]
    args.append(nc.dram_tensor("out_dram", (B, T, D), F32, kind="ExternalOutput").ap())
    two_layers(nc, *args)
    return run(nc, [arrays], core_ids=[0]).results[0]["out_dram"]
```

```python
from contextlib import ExitStack

import concourse.bass as bass
from concourse import mybir

P = 128
B, T, D = 2, 1024, 512
H, DH = 16, 32
HG = P // DH
NG = H // HG
KC = D // P
RT = T // P
W = 512
NC = T // W
TPC = W // P
F0, F1 = 2048, 1408
CH = (F0 // P, F1 // P)
PAIRS = (2, 1)
EPS = 1e-5
SCALE = float(DH) ** -0.5
MASKED = -1e38
STACK = 3 * DH
SHIFT = STACK + 2

F32, F32R, BF16 = mybir.dt.float32, mybir.dt.float32r, mybir.dt.bfloat16
ALU = mybir.AluOpType
ACT = mybir.ActivationFunctionType
AX = mybir.AxisListType



NAT = [(qb, part, (min(qb + 1, TPC) if part == 0 else qb + 1 - TPC) * P)
       for qb in range(RT) for part in range(1 + (qb >= TPC))]
SETS = [(c, kb) for c in range(NC) for kb in range(TPC * (c + 1))]


GU_PARTS = 3


def mlp(layer, sizes):
    out, downs = [], []
    for j, nfc in enumerate(sizes):
        for blk in range(NC):
            for fc in range(nfc):
                last = blk == NC - 1 and fc == nfc - 1
                out += [[("part", "gate", j, blk, fc, k)] for k in range(GU_PARTS - 1)]
                out.append([("gate", j, blk, fc, nfc)] + [("w", "G")] * last)
                out, downs = out + downs, []
                out += [[("part", "up", j, blk, fc, k)] for k in range(GU_PARTS - 1)]
                out.append([("up", j, blk, fc, nfc), ("gated", j, blk, fc, nfc)] + [("w", "U")] * last)
            for i in range(TPC):
                downs.append([("down", j, blk, i, nfc), ("add_down", j, blk, i, nfc)])
            if blk == NC - 1:
                downs[-1].append(("w", "D"))
    return out + downs


def natural():
    return [[("nat", h, u)] for h in range(HG) for u in range(len(NAT))]


def weighted():
    st = [[[("st", 0, h) for h in two] for two in ((0, 1), (2, 3))]]
    for i in range(1, len(SETS) + 1):
        scores = [("st", i, h) for h in range(HG)] if i < len(SETS) else []
        now = [scores[:2] + [("pv", i - 1)], scores[2:] + [("sums", i - 1)]]
        c, kb = SETS[i - 1]
        if kb == TPC * (c + 1) - 1:
            now[-1].append(("heads", c))
        st.append(now)
    return st


def projections():
    proj = [[("proj", t)] + [("rotate", t - 1)] * (t > 0) for t in range(2 * NC)]
    proj.append([("rotate", 2 * NC - 1)])
    proj[0].insert(0, ("v_slice", 1))
    return proj


def output(c):
    return [[("wo", c, i), ("add_wo", c, i)] for i in range(TPC)]


def norms(layer, tiles):
    out = []
    for k, rt in enumerate(tiles):
        now = [("xn", layer, rt)] if k == 0 else []
        now += [("xn", layer, tiles[k + 1])] if k + 1 < len(tiles) else []
        out.append(now + [("norm", rt)])
    return out


FILL = {"turn0": (8, 26, 8, 4), "turn1": (5, 14, 4, 4), "tail0": (10, 23, 8, 14), "tail1": (7, 30, 8, 10)}
ENDS = ("rrppsxpxpxxpwwwwD", "rprpsxpxpxxpwwwwD")
LATE = {"turn0": (1, 2, 9, 2, 0), "turn1": (3, 3, 6, 2, 0), "tail0": (2, 4, 5, 2, 0), "tail1": (0, 2, 6, 2, 0)}
SPLIT = {"turn0": 3, "turn1": 2, "tail0": 1, "tail1": 4}
SHARES = {"turn0": (2, 2), "turn1": (2,), "tail0": (2, 2), "tail1": (2, 2, 1)}


def turn(layer, tail):
    name = ("turn", "tail")[tail] + str(layer)
    pieces = mlp(layer, SHARES[name])
    a, b, c, d = FILL[name]
    e = len(pieces) - a - b - c - d
    take = iter(pieces)

    def some(k):
        return [next(take) for _ in range(k)]
    out = ([[("v_load", 1 - layer)]] if tail else []) + some(a)
    nat = merged(natural(), some(b))
    if layer == 0:
        nat.insert(20, [("w", "A")])
        nat.append([("w", "O")])
    else:
        nat.insert(8, [("w", "O")])
        nat.insert(28, [("w", "A")])
    out += nat + some(SPLIT[name]) + [[("shift",)]] + some(c - SPLIT[name])
    st = weighted()
    r, q, w_, f, g = LATE[name]
    fill = some(2)
    out += st[0][:1] + fill[:1] + st[0][1:] + fill[1:] + merged([p for s in st[1:TPC + 1] for p in s], some(g))
    late = [p for s in st[TPC + 1:] for p in s]
    recip = [[("recip", 0, 0)], [("recip", 0, 1), ("scaled", 0)]]
    late = late[:r] + recip[:1] + late[r:q] + recip[1:] + late[q:w_] + output(0) + late[w_:]
    out += some(f) + merged(late, some(e - 2 - f - g))
    if not tail:
        kinds = {"p": iter(projections()), "x": iter(some(d)), "w": iter(output(1)),
                 "r": iter([[("recip", 1, 0)], [("recip", 1, 1)]]), "s": iter([[("scaled", 1)]])}
        end = [next(kinds[k]) if k in kinds else [("split", k)] for k in ENDS[layer]]
        out += [[("w", s[1]) if s[0] == "split" else s for s in piece if s[0] != "w"] for piece in end]
        return [s for piece in out for s in piece]
    chain = [[("recip", 1, 0)], [("recip", 1, 1)], [("scaled", 1)]]
    rest = some(d)
    if layer == 0:
        out += merged(chain, rest[:10]) + output(1) + [[("stats", 1, 0)]] + rest[10:11]
        out += merged([[("v_weights", 1)]] + norms(1, range(TPC)), rest[11:])
    else:
        out += merged(chain, rest[:6]) + [[("store", 0)], [("x_next",)]] + merged(output(1), rest[6:]) + [[("store", 1)]]
    return [s for piece in out for s in piece]


def merged(a, b):
    out, k = [], 0
    for i, piece in enumerate(a):
        out.append(piece)
        while k < len(b) and (k + 1) * len(a) <= (i + 1) * len(b):
            out.append(b[k])
            k += 1
    return out + b[k:]


def opening(layer):
    out = []
    if layer == 0:
        out = [("stats", 0, 0), ("v_weights", 0)] + [x for piece in norms(0, range(TPC)) for x in piece] + [("keep", 0)]
    proj = [("proj", t) for t in range(2 * NC)]
    values = [("values", rt) for rt in range(RT)]
    later = norms(layer, range(TPC, RT))
    out += [("stats", layer, 1)] + ([proj[0], values[0]], [values[0], proj[0]])[layer] + [values[1]] + later[0] + [values[2]] + later[1] + [values[3]]
    out += later[2] + later[3] + [("keep", 1)] * (layer == 0)
    out += [values[4], ("rotate", 0), proj[1], values[5], ("rotate", 1), proj[2], values[6], ("rotate", 2), proj[3], values[7],
            ("rotate", 3)]
    for k, x in enumerate(out):
        if x[0] == "values":
            out[k] = x + (max(0, sum(y[0] == "norm" and y[1] >= TPC for y in out[:k]) - max(0, x[1] + 1 - TPC)),)
    return out + [("v_slice", 0)]


ADDS = {
    "v_load": {"d_wv": 16},
    "v_weights": {"d_rope": 16, "v_wv": 1, "g_wv": 1},
    "stats": {"v_chain": 2 * TPC + 5, "v_var": 1, "a_std": 1},
    "keep": {"a_keep": 1},
    "x_next": {"d_x0": 16, "d_x1": 16},
    "xn": {"v_xn": 1},
    "norm": {"p_xt": 1, "a_xh": 1, "v_dfree": 1},
    "values": {"p_v": 1, "a_val": 1},
    "v_slice": {"d_v": 16},
    "proj": {"p_proj": 1, "v_cos": 1, "v_swap": 1, "g_sin": 1},
    "rotate": {"v_rope": 1, "a_rh": 1, "g_rl": 1},
    "nat": {"p_nat": 1, "v_max": 1},
    "shift": {"v_chain": 2, "v_m": 1, "p_shift": 1, "v_shift": 1, "d_shift": 32},
    "st": {"p_st": 1, "a_exp": 1},
    "pv": {},
    "sums": {"p_pv": 1},
    "heads": {"a_heads": 1},
    "recip": {"v_recip": 1},
    "scaled": {"v_heads": 1, "a_ah": 1, "g_al": 1},
    "wo": {"p_wo": 1},
    "add_wo": {"v_dfree": 1},
    "part": {},
    "gate": {"p_gate": 1, "a_tanh": 1},
    "up": {"p_up": 1},
    "gated": {"v_gate": 1, "v_h": 1, "a_hh": 1, "g_hl": 1},
    "down": {"p_down": 1},
    "add_down": {"v_dfree": 1},
    "w": {"a_hi": 1, "g_lo": 1},
    "store": {},
}
STACKS = 3 * 16

SLOTS = {"open0": "", "turn0": "A0 G1 U0 O1 D0 G1 U0 D1", "tail0": "A0 G1 U0 O1 D0 G1 U0 D1",
         "open1": "", "turn1": "O1 A0 G0 U1 D0", "tail1": "O1 A0 G1 U0 D1 G0 U1 D0 G1 U0 D1"}
SPLITS_OPEN = "ADGU"

SEMS = sorted({x for a in ADDS.values() for x in a} | {"raw0", "g_ds", "raw1", "d_x0", "d_x1", "d_out"} | {f"d_stack{h}" for h in range(HG)})
CREDIT = {s: 0 if s[0] == "d" or s[:3] == "raw" else 1 for s in SEMS}
CREDIT.update(v_dfree=2, g_hl=2, d_out=16)


class Count:

    def __init__(self):
        self.n = dict(CREDIT)
        self.n["a_hi"] += len(SPLITS_OPEN)
        self.n["g_lo"] += len(SPLITS_OPEN)
        self.n["raw0"] += 16
        self.loops = []
        self.bases = {}
        self.split = 0
        self.d = 0

    def dk(self):
        self.d += 1
        return (self.d - 1) % 2

    def ready(self, kind):
        return self.base("g_lo") + self.w_ready[kind]

    def __call__(self, sem, k=0):
        return self.base(sem) + (self.n[sem] + k)

    def base(self, sem):
        if sem not in self.bases:
            v = 0
            for i, per in self.loops:
                v = i * per[sem] + v
            self.bases[sem] = self.eng.snap(v)
        return self.bases[sem]

    def did(self, step, region):
        for sem, k in ADDS[step[0]].items():
            self.n[sem] += k
        if step[0] == "proj" and step[1] % NC == NC - 1:
            for h in range(HG):
                self.n[f"d_stack{h}"] += STACKS
        if step[0] == "w":
            self.n["g_ds"] += SCALED[region, self.split]
            self.n[f"raw{PLAN[region][self.split][0]}"] += 16
            self.split += 1
        if step[0] == "store":
            self.n["d_out"] += 16


def total(parts):
    c = Count()
    before = dict(c.n)
    for region, steps, times in parts:
        for _ in range(times):
            c.split = 0
            for s in steps:
                c.did(s, region)
    return {k: c.n[k] - before[k] for k in c.n}


REGIONS = []
for _l in (0, 1):
    REGIONS += [(f"open{_l}", opening(_l), 1), (f"turn{_l}", turn(_l, False), NG - 1), (f"tail{_l}", turn(_l, True), 1)]
LAYER = {region: int(region[-1]) for region, _, _ in REGIONS}
MLP_STEP = {"turn0": 2 * PAIRS[0], "turn1": 2 * PAIRS[1]}


def plan_loads():
    seq = []
    at = {"A": 0, "O": -1, "G": 0, "U": 0, "D": 0}
    for b in range(2):
        size = {k: [w_ for l in (0, 1) for w_ in SIZES_OF[l]] for k in "GUD"}
        for region, steps, times in REGIONS:
            kinds = [s[1] for s in steps if s[0] == "w"]
            slots = SLOTS[region].split()
            assert kinds == [x[0] for x in slots], (region, kinds)
            for g in range(times):
                for k, x in enumerate(slots):
                    at[x[0]] += size[x[0]].pop(0) if x[0] in size else 1
                    seq.append((region, g, k, x[0], int(x[1]), at[x[0]]))
    plan, scaled = {}, {}
    for i, (region, g, k, kind, slot, own) in enumerate(seq[:len(seq) // 2]):
        nxt = next(x for x in seq[i + 1:] if x[4] == slot)
        step = 1 if nxt[3] in "AO" else MLP_STEP.get(region, 0)
        entry = (slot, nxt[3], nxt[5] - g * step)
        row = plan.setdefault(region, [])
        if g == 0:
            row.append(entry)
        assert row[k] == entry, (region, g, k, row[k], entry)
        is_scaled = kind == "D" and CH[0] <= own < sum(CH)
        assert scaled.setdefault((region, k), is_scaled) == is_scaled
    return plan, scaled


SIZES_OF = tuple(SHARES[f"turn{_l}"] * (NG - 1) + SHARES[f"tail{_l}"] for _l in (0, 1))
PLAN, SCALED = plan_loads()


def last_splits(region):
    names = [r for r, _, _ in REGIONS]
    i = names.index(region)
    ways = [[x for r in names[:i] for x in SLOTS[r].split()]]
    if i == 0:
        ways = [[x for r in names for x in SLOTS[r].split()]]
    if REGIONS[i][2] > 1:
        ways.append(ways[0] + SLOTS[region].split())
    ways = [list(SPLITS_OPEN) + w_ for w_ in ways]
    if i == 0:
        ways.append(list(SPLITS_OPEN))
    ways = ["".join(x[0] for x in w_) for w_ in ways]
    return {k: min(len(w_) - 1 - w_.rfind(k) if k in w_ else 0 for w_ in ways) for k in "AOGUD"}
PER_BATCH = total(REGIONS)


def two_layers(nc, x, wqk, wo, wv, wgate, wup, wdown, rope, scales, down_s, out):
    ctx = ExitStack()
    with ctx:
        def sb(name, shape, dt=F32):
            return ctx.enter_context(nc.sbuf_tensor(name, shape, dt))

        def bank(name):
            return ctx.enter_context(nc.psum_tensor(name, [P, W], F32))

        sem = {s: ctx.enter_context(nc.semaphore(s)) for s in SEMS}
        s_const = ctx.enter_context(nc.semaphore("s_const"))
        d_const = ctx.enter_context(nc.semaphore("d_const"))
        s_vconst = ctx.enter_context(nc.semaphore("s_vconst"))

        xres = sb("xres", [P, RT, D])
        xh, xl = sb("xh", [P, KC, T], F32R), sb("xl", [P, KC, T], F32R)
        val = sb("val", [P, RT, D])
        vh = sb("vh", [P, RT, P])
        raw = sb("raw", [P, 2, 2 * W])
        wqkh, wqkl = sb("wqkh", [P, 2, KC, P], F32R), sb("wqkl", [P, 2, KC, P], F32R)
        woh, wol = sb("woh", [P, D], F32R), sb("wol", [P, D], F32R)
        wgh, wgl = sb("wgh", [P, 2, KC, P], F32R), sb("wgl", [P, 2, KC, P], F32R)
        wuh, wul = sb("wuh", [P, 2, KC, P], F32R), sb("wul", [P, 2, KC, P], F32R)
        wdh, wdl = sb("wdh", [P, 2, D], F32R), sb("wdl", [P, 2, D], F32R)
        QS, KS = sb("QS", [P, HG, T], F32R), sb("KS", [P, HG, T], F32R)
        wvh = QS[:, 0:2, :].rearrange("p a (b n) -> p (a b) n", n=D)
        wvl = QS[:, 2:4, :].rearrange("p a (b n) -> p (a b) n", n=D)
        swapped = sb("swapped", [P, 2, W])
        trig = sb("trig", [P, 2, T])
        wv_raw = trig[:, :, :].rearrange("p a (b n) -> p (a b) n", n=D)
        pr = sb("pr", [P, 8, W])
        flat_h = [pr[:, 2 * NC * k:2 * NC * k + NC, :].rearrange("p c n -> p (c n)") for k in range(2)]
        flat_l = [pr[:, 2 * NC * k + NC:2 * NC * (k + 1), :].rearrange("p c n -> p (c n)") for k in range(2)]
        xn = sb("xn", [P, 2, D])
        heads, denom = sb("heads", [P, W]), sb("denom", [P, W])
        ah, al = sb("ah", [P, W], F32R), sb("al", [P, W], F32R)
        tt = sb("tt", [P, 2, W])
        hh, hl = sb("hh", [P, 2, W], F32R), sb("hl", [P, 2, W], F32R)
        ds = sb("ds", [P, D])
        ident = sb("ident", [P, P])
        ident_b = sb("ident_b", [P, P], BF16)
        mask_q, mask_k = sb("mask_q", [P, P], BF16), sb("mask_k", [P, P], BF16)
        ones = sb("ones", [P, DH])
        mp = sb("mp", [P, HG * RT, 2])
        mx = sb("mx", [P, HG * RT])
        mm = sb("mm", [P, P // (HG * RT), HG * RT])
        mt = sb("mt", [2 * HG * RT, P], F32R)
        stat6 = sb("stat6", [P, RT, 6])
        mv = sb("mv", [P, RT, 2])
        st = sb("st", [P, NC, 6, TPC])
        sc = sb("sc", [P, CH[1], 2])
        half_gs, both_s = sb("half_gs", [P, CH[1]]), sb("both_s", [P, CH[1]])

        S = [bank("S0"), bank("S1")]
        G, U = bank("G"), bank("U")
        Dk = [bank("D0"), bank("D1")]
        O, E = bank("O"), bank("E")
        NB = S + [O, E]

        SPLIT_TO = {"A": (wqkh, wqkl), "O": (woh, wol), "G": (wgh, wgl), "U": (wuh, wul), "D": (wdh, wdl)}
        SIZE = {"A": 2 * W, "O": W, "G": 2 * W, "U": 2 * W, "D": 2 * W}
        FREED_BY = {"A": "p_proj", "O": "p_wo", "G": "p_gate", "U": "p_up", "D": "p_down"}

        def flat(t):
            return t[:, :] if len(t.shape) == 2 else t[:, :, :].rearrange("p a b -> p (a b)") \
                if len(t.shape) == 3 else t[:, :, :, :].rearrange("p a b c -> p (a b c)")

        FIRST = {"A": raw[:, 0, :], "D": tt[:, :, :].rearrange("p a b -> p (a b)"),
                 "G": pr[:, 4:6, :].rearrange("p a b -> p (a b)"), "U": pr[:, 6:8, :].rearrange("p a b -> p (a b)")}
        d_first = {k: ctx.enter_context(nc.semaphore(f"d_first_{k}")) for k in SPLITS_OPEN[1:]}

        def load(sp, kind, at, dst, done):
            dst = dst[:, 0:SIZE[kind]]
            if kind in "AO":
                src = (wqk if kind == "A" else wo)[bass.ds(at, 1), :, :].rearrange("a p n -> p (a n)")
            else:
                src = {"G": wgate, "U": wup, "D": wdown}[kind][bass.ds(at, 2), :, :].rearrange("a p n -> p a n")
                dst = dst.rearrange("p (a n) -> p a n", a=2)
            sp.dma_start(dst, src).then_inc(sem[done] if done else d_first[kind], 16)

        def walk(eng, part):
            with eng.Fori(0, B) as b:
                n = Count()
                n.eng, n.b = eng, b
                n.loops.append((b, PER_BATCH))
                n.part = part
                for region, steps, times in REGIONS:
                    n.region, n.layer = region, LAYER[region]
                    n.split, n.d, n.turns = 0, 0, NG - 1 if region[:4] == "tail" else 0
                    n.turns_w = 0
                    n.w_ready = {k: n.n["g_lo"] - d for k, d in last_splits(region).items()}
                    n.bases = {}
                    if times == 1:
                        walk_steps(n, steps)
                        continue
                    start = dict(n.n)
                    with eng.Fori(0, times) as g:
                        per = total([(region, steps, 1)])
                        n.loops.append((g, per))
                        n.bases = {}
                        n.turns = n.turns_w = g
                        walk_steps(n, steps)
                        n.loops.pop()
                    for k in start:
                        n.n[k] = start[k] + times * (n.n[k] - start[k])

        def walk_steps(n, steps):
            for s in steps:
                if s[0] in n.part:
                    n.part[s[0]](n, *s[1:])
                n.did(s, n.region)
                if s[0] == "w":
                    n.w_ready[s[1]] = n.n["g_lo"]

        def chunk(n, j, fc):
            at = n.turns * (2 * PAIRS[1]) + (2 * j + fc)
            return bass.ds(at, 1)

        def proj_bank(n, t):
            return S[t % 2] if n.region[:4] == "open" else NB[t]

        block = ctx.enter_context(nc.Block())

        @block.sync
        def _(sp):
            for s in SEMS:
                if CREDIT[s]:
                    sp.sem_inc(sem[s], CREDIT[s])
            sp.dma_start(sc[:, :, :], scales).then_inc(d_const, 16)
            sp.dma_start(ds[:, :], down_s).then_inc(d_const, 16)
            def first_rows(c):
                sp.dma_start(val[:, c * TPC:(c + 1) * TPC, :], x[0, c * W:(c + 1) * W, :].rearrange("(t p) d -> p t d", p=P)) \
                    .then_inc(sem[f"d_x{c}"], 16)

            first_rows(0)
            load(sp, "A", 0, raw[:, 0, :], "raw0")
            sp.dma_start(wv_raw, wv[0].rearrange("p (c n) -> p c n", c=KC)).then_inc(sem["d_wv"], 16)
            for kind in SPLITS_OPEN[1:]:
                load(sp, kind, 0, FIRST[kind], None)
            first_rows(1)
            load(sp, "G", 2, raw[:, 1, :], "raw1")
            sp.wait_ge(sem["g_lo"], CREDIT["g_lo"] + 1)
            load(sp, "A", 1, raw[:, 0, :], "raw0")

            def v_load(n, layer):
                sp.wait_ge(sem["g_rl"], n("g_rl"))
                sp.dma_start(wv_raw, wv[layer].rearrange("p (c n) -> p c n", c=KC)).then_inc(sem["d_wv"], 16)

            def v_weights(n, layer):
                sp.wait_ge(sem["g_wv"], n("g_wv", 1))
                sp.dma_start(trig[:, :, :], rope[layer]).then_inc(sem["d_rope"], 16)

            def rows(dram, n, c):
                return dram[bass.ds(n.b, 1), c * W:(c + 1) * W, :].rearrange("a (t p) d -> p (a t) d", p=P)

            def x_next(n):
                sp.wait_ge(sem["d_v"], n("d_v"))
                for c in range(NC):
                    sp.dma_start(val[:, c * TPC:(c + 1) * TPC, :],
                                 x[bass.ds(n.b + 1, 1), c * W:(c + 1) * W, :].rearrange("a (t p) d -> p (a t) d", p=P)) \
                        .then_inc(sem[f"d_x{c}"], 16)

            def v_slice(n, ahead):
                sp.wait_ge(sem["p_pv"], n("p_pv"))
                sp.wait_ge(sem["a_val"], n("a_val"))
                sp.dma_start(vh[:, :, :], val[:, :, bass.ds((n.turns + ahead) * P, P)]).then_inc(sem["d_v"], 16)

            def rotate(n, t):
                if t % NC < NC - 1:
                    return
                qk = t // NC
                flats = ((flat_h, flat_h, flat_l), (flat_h, flat_l, flat_h))[qk]
                sp.wait_ge(sem["g_rl"], n("g_rl", 1))
                if n.region[:4] == "open" and qk:
                    sp.wait_ge(sem["p_v"], n("p_v"))
                for h in range(HG):
                    for r, src in enumerate(flats):
                        sp.dma_start((KS, QS)[qk][r * DH:(r + 1) * DH, h, :].bitcast(F32),
                                     src[qk][h * DH:(h + 1) * DH, :]).then_inc(sem[f"d_stack{h}"], 16)

            def shift(n):
                sp.wait_ge(sem["v_shift"], n("v_shift", 1))
                for k in range(2):
                    sp.dma_start(QS[STACK + k:STACK + k + 1, :, :].rearrange("o h (q n) -> o (h q) n", n=P).bitcast(F32),
                                 mt[k * HG * RT:(k + 1) * HG * RT, :].bitcast(F32)).then_inc(sem["d_shift"], 16)

            def w(n, kind):
                slot, nxt, at = PLAN[n.region][n.split]
                sp.wait_ge(sem["g_lo"], n("g_lo", 1))
                load(sp, nxt, n.turns_w * (1 if nxt in "AO" else MLP_STEP.get(n.region, 0)) + at, raw[:, slot, :], f"raw{slot}")

            def store(n, c):
                sp.wait_ge(sem["v_dfree"], n("v_dfree"))
                sp.dma_start(rows(out, n, c), xres[:, c * TPC:(c + 1) * TPC, :]).then_inc(sem["d_out"], 16)

            walk(sp, dict(v_load=v_load, v_weights=v_weights, x_next=x_next, v_slice=v_slice, rotate=rotate, shift=shift, w=w, store=store))
            sp.wait_ge(sem["d_out"], CREDIT["d_out"] + 16 * NC * B)
            for k in range(2):
                sp.wait_ge(sem[f"raw{k}"], 16 * (k == 0) + B * PER_BATCH[f"raw{k}"] + 16)
            for c in range(NC):
                sp.wait_ge(sem[f"d_x{c}"], 16 * (B + 1))
            sp.wait_ge(sem["d_wv"], 16 * (2 * B + 1))

        @block.scalar
        def _(act):
            def stats(n, layer, c):
                act.wait_ge(sem["v_var"], n("v_var", 1))
                act.activation(st[:, c, 1, :], st[:, c, 0, :], ACT.Sqrt).then_inc(sem["a_std"], 1)

            def keep(n, c):
                act.wait_ge(sem[f"d_x{c}"], n(f"d_x{c}", 16))
                act.wait_ge(sem["d_out"], n("d_out"))
                act.copy(xres[:, c * TPC:(c + 1) * TPC, :], val[:, c * TPC:(c + 1) * TPC, :]) \
                    .then_inc(sem["a_keep"], 1)

            def norm(n, rt):
                act.wait_ge(sem["p_xt"], n("p_xt", 1))
                act.copy(xh[:, :, rt * P:(rt + 1) * P], Dk[n.dk()][:, :].rearrange("p (c n) -> p c n", c=KC)) \
                    .then_inc(sem["a_xh"], 1)

            def values(n, rt, behind):
                act.wait_ge(sem["p_v"], n("p_v", 1))
                if n.layer == 0 and rt % TPC == 0:
                    act.wait_ge(sem["a_keep"], n("a_keep"))
                act.copy(val[:, rt, :], (O, E)[rt % 2][:, :]).then_inc(sem["a_val"], 1)

            def other_bank(n, *_):
                n.dk()

            def rotate(n, t):
                act.wait_ge(sem["v_rope"], n("v_rope", 1))
                cols = slice((t % NC) * W, (t % NC + 1) * W)
                act.copy(flat_h[t // NC][:, cols].bitcast(F32R), flat_l[t // NC][:, cols]).then_inc(sem["a_rh"], 1)

            def st_(n, i, h):
                c, kb = SETS[i]
                skip = max(0, kb - TPC * c) * P
                act.wait_ge(sem["p_st"], n("p_st", 1))
                act.wait_ge(sem["p_pv"], n("p_pv"))
                act.activation(pr[:, (i * HG + h) % 8, skip:W], S[h % 2][:, skip:W], ACT.Exp, scale=SCALE) \
                    .then_inc(sem["a_exp"], 1)

            def heads_(n, c):
                act.wait_ge(sem["p_pv"], n("p_pv"))
                act.wait_ge(sem["g_al"], n("g_al"))
                act.copy(heads[:, :], O[:, :])
                act.copy(denom[:, :], E[:, :]).then_inc(sem["a_heads"], 1)

            def scaled(n, c):
                act.wait_ge(sem["v_heads"], n("v_heads", 1))
                act.wait_ge(sem["p_wo"], n("p_wo"))
                act.copy(ah[:, :], heads[:, :]).then_inc(sem["a_ah"], 1)

            def gate(n, j, blk, fc, nfc):
                act.wait_ge(sem["p_gate"], n("p_gate", 1))
                act.wait_ge(sem["g_hl"], n("g_hl", -1))
                par = (blk * nfc + fc) % 2
                act.activation(tt[:, par, :], G[:, :], ACT.Tanh,
                               scale=half_gs[:, chunk(n, j, fc)] if n.layer else 0.5).then_inc(sem["a_tanh"], 1)

            def gated(n, j, blk, fc, nfc):
                act.wait_ge(sem["v_h"], n("v_h", 1))
                act.wait_ge(sem["p_down"], n("p_down"))
                act.copy(hh[:, fc, :], tt[:, (blk * nfc + fc) % 2, :]).then_inc(sem["a_hh"], 1)

            def high(kind, src):
                return act.copy(flat(SPLIT_TO[kind][0]), src[:, 0:SIZE[kind]])

            def w(n, kind):
                slot = PLAN[n.region][n.split][0]
                act.wait_ge(sem[f"raw{slot}"], n(f"raw{slot}", 16))
                act.wait_ge(sem[FREED_BY[kind]], n(FREED_BY[kind]))
                if SCALED[n.region, n.split]:
                    act.wait_ge(sem["g_ds"], n("g_ds", 1))
                high(kind, raw[:, slot, :]).then_inc(sem["a_hi"], 1)

            for kind in SPLITS_OPEN:
                act.wait_ge(sem["raw0"] if kind == "A" else d_first[kind], 16)
                high(kind, FIRST[kind]).then_inc(sem["a_hi"], 1)
            act.wait_ge(s_vconst, 2)
            walk(act, dict(stats=stats, keep=keep, norm=norm, values=values, rotate=rotate, st=st_, heads=heads_, gate=gate,
                           gated=gated, scaled=scaled, down=other_bank, wo=other_bank, w=w))

        @block.gpsimd
        def _(pool):
            pool.wait_ge(d_const, 32)
            pool.memset(ident[:, :], 1.0).then_inc(s_const, 1)
            pool.memset(ident_b[:, :], 1.0).then_inc(s_const, 1)
            pool.memset(mask_q[:, :], 0.0).then_inc(s_const, 1)
            pool.memset(mask_k[:, :], 0.0).then_inc(s_const, 1)
            pool.wait_ge(s_const, 4)
            for t in (ident, ident_b):
                pool.affine_select(out=t[:, :], in_=t[:, :], pattern=[[1, P]], compare_op=ALU.is_equal, fill=0.0,
                                   base=0, channel_multiplier=-1).then_inc(s_const, 1)
            pool.affine_select(out=mask_q[:, :], in_=mask_q[:, :], pattern=[[-1, P]], compare_op=ALU.is_ge,
                               fill=MASKED, base=0, channel_multiplier=1).then_inc(s_const, 1)
            pool.affine_select(out=mask_k[:, :], in_=mask_k[:, :], pattern=[[1, P]], compare_op=ALU.is_ge,
                               fill=MASKED, base=0, channel_multiplier=-1).then_inc(s_const, 1)

            def low(kind, src):
                hi, lo = SPLIT_TO[kind]
                return pool.tensor_tensor(flat(lo), src[:, 0:SIZE[kind]], flat(hi).bitcast(F32), ALU.subtract)

            for i, kind in enumerate(SPLITS_OPEN):
                pool.wait_ge(sem["a_hi"], CREDIT["a_hi"] + i + 1)
                low(kind, FIRST[kind]).then_inc(sem["g_lo"], 1)

            def v_weights(n, layer):
                pool.wait_ge(sem["v_wv"], n("v_wv", 1))
                pool.tensor_tensor(wvl, wv_raw, wvh.bitcast(F32), ALU.subtract).then_inc(sem["g_wv"], 1)

            def w(n, kind):
                slot = PLAN[n.region][n.split][0]
                if SCALED[n.region, n.split]:
                    pool.wait_ge(sem[f"raw{slot}"], n(f"raw{slot}", 16))
                    for fc in range(2):
                        half = raw[:, slot, fc * D:(fc + 1) * D]
                        ins = pool.tensor_tensor(half, half, ds[:, :], ALU.mult)
                    ins.then_inc(sem["g_ds"], 1)
                pool.wait_ge(sem["a_hi"], n("a_hi", 1))
                low(kind, raw[:, slot, :]).then_inc(sem["g_lo"], 1)

            def gated(n, j, blk, fc, nfc):
                pool.wait_ge(sem["a_hh"], n("a_hh", 1))
                pool.tensor_tensor(hl[:, fc, :], tt[:, (blk * nfc + fc) % 2, :], hh[:, fc, :].bitcast(F32), ALU.subtract) \
                    .then_inc(sem["g_hl"], 1)

            def proj(n, t):
                pool.wait_ge(sem["v_swap"], n("v_swap", 1))
                sw = swapped[:, t % 2, :]
                pool.tensor_tensor(sw, sw, trig[:, 1, (t % NC) * W:(t % NC + 1) * W], ALU.mult).then_inc(sem["g_sin"], 1)

            def rotate(n, t):
                pool.wait_ge(sem["a_rh"], n("a_rh", 1))
                cols = slice((t % NC) * W, (t % NC + 1) * W)
                lo = flat_l[t // NC][:, cols]
                pool.tensor_tensor(lo.bitcast(F32R), lo, flat_h[t // NC][:, cols], ALU.subtract).then_inc(sem["g_rl"], 1)

            def scaled(n, c):
                pool.wait_ge(sem["a_ah"], n("a_ah", 1))
                pool.tensor_tensor(al[:, :], heads[:, :], ah[:, :].bitcast(F32), ALU.subtract).then_inc(sem["g_al"], 1)

            walk(pool, dict(v_weights=v_weights, w=w, gated=gated, proj=proj, rotate=rotate, scaled=scaled))

        @block.vector
        def _(dve):
            dve.memset(ones[:, :], 1.0)
            dve.memset(mp[:, :, :], -3e38)
            dve.memset(mm[:, :, :], 0.0)
            dve.memset(KS[STACK:P, :, :].bitcast(F32), 1.0)
            dve.wait_ge(d_const, 32)
            dve.tensor_scalar(half_gs[:, :], sc[:, :, 0], 0.5, None, ALU.mult).then_inc(s_vconst, 1)
            dve.wait_ge(s_vconst, 1)
            dve.tensor_tensor(both_s[:, :], half_gs[:, :], sc[:, :, 1], ALU.mult).then_inc(s_vconst, 1)
            dve.wait_ge(s_vconst, 2)
            def linker(n):
                k = [0]

                def link(ins, ordered=True):
                    k[0] += 1
                    ins.then_inc(sem["v_chain"], 1)
                    if ordered:
                        dve.wait_ge(sem["v_chain"], n("v_chain", k[0]))
                return link

            def v_weights(n, layer):
                dve.wait_ge(sem["d_wv"], n("d_wv", 16))
                dve.wait_ge(sem["p_st"], n("p_st"))
                dve.tensor_copy(wvh, wv_raw).then_inc(sem["v_wv"], 1)

            def stats(n, layer, c):
                link = linker(n)
                if layer == 0:
                    dve.wait_ge(sem[f"d_x{c}"], n(f"d_x{c}", 16))
                else:
                    dve.wait_ge(sem["v_dfree"], n("v_dfree"))
                tiles = range(c * TPC, (c + 1) * TPC)
                t = st[:, c]
                for rt in tiles:
                    link(dve.bn_stats(stat6[:, rt, :], (xres if layer else val)[:, rt, :]), rt == tiles[-1])
                dve.memset(t[:, 2, :], 0.0)
                for rt in tiles:
                    link(dve.bn_aggr(mv[:, rt, :], stat6[:, rt, :]), rt == tiles[-1])
                dve.tensor_scalar(t[:, 0, :], mv[:, tiles[0]:tiles[-1] + 1, 1], EPS, None, ALU.add).then_inc(sem["v_var"], 1)
                dve.wait_ge(sem["v_var"], n("v_var", 1))
                dve.wait_ge(sem["a_std"], n("a_std", 1))
                link(dve.reciprocal(t[:, 2, :], t[:, 1, :]))
                link(dve.tensor_tensor(t[:, 3, :], t[:, 0, :], t[:, 2, :], ALU.mult))
                link(dve.tensor_tensor(t[:, 4, :], t[:, 3, :], t[:, 1, :], ALU.add))
                link(dve.reciprocal(t[:, 3, :], t[:, 4, :]))
                link(dve.tensor_scalar(t[:, 5, :], t[:, 3, :], 2.0, None, ALU.mult))

            def xn_(n, layer, rt):
                dve.wait_ge(sem["p_xt"], n("p_xt", -1 if rt % TPC > 1 else 0))
                dve.tensor_scalar(xn[:, rt % 2, :], (xres if layer else val)[:, rt, :], mv[:, rt, 0:1],
                                  st[:, rt // TPC, 5, rt % TPC:rt % TPC + 1], ALU.subtract, ALU.mult).then_inc(sem["v_xn"], 1)

            def norm(n, rt):
                dve.wait_ge(sem["a_xh"], n("a_xh", 1))
                dve.tensor_tensor(xl[:, :, rt * P:(rt + 1) * P],
                                  Dk[n.dk()][:, :].rearrange("p (c n) -> p c n", c=KC),
                                  xh[:, :, rt * P:(rt + 1) * P].bitcast(F32), ALU.subtract) \
                    .then_inc(sem["v_dfree"], 1)

            def proj(n, t):
                cols = slice((t % NC) * W, (t % NC + 1) * W)
                if t == 0:
                    dve.wait_ge(sem["d_rope"], n("d_rope"))
                dve.wait_ge(sem["p_proj"], n("p_proj", 1))
                src = proj_bank(n, t)
                dve.wait_ge(sem["v_rope"], n("v_rope"))
                dve.tensor_tensor(flat_l[t // NC][:, cols], src[:, :], trig[:, 0, cols], ALU.mult).then_inc(sem["v_cos"], 1)
                dve.stream_shuffle(swapped[:, t % 2, :], src[:, :], [i ^ 1 for i in range(32)]).then_inc(sem["v_swap"], 1)

            def rotate(n, t):
                turned = flat_l[t // NC][:, (t % NC) * W:(t % NC + 1) * W]
                ahead = -1 if n.region[:4] == "turn" and t < 2 * NC - 1 else 0
                dve.wait_ge(sem["v_cos"], n("v_cos", ahead))
                dve.wait_ge(sem["g_sin"], n("g_sin", ahead))
                dve.tensor_tensor(turned, turned, swapped[:, t % 2, :], ALU.add).then_inc(sem["v_rope"], 1)

            def nat(n, h, u):
                qb, part, w_ = NAT[u]
                dve.wait_ge(sem["p_nat"], n("p_nat", 1))
                dve.tensor_reduce(mp[:, h * RT + qb, part:part + 1], NB[(h * len(NAT) + u) % 4][:, 0:w_], AX.X, ALU.max) \
                    .then_inc(sem["v_max"], 1)

            def shift(n):
                link = linker(n)
                dve.wait_ge(sem["v_max"], n("v_max"))
                link(dve.tensor_reduce(mx[:, :], mp[:, :, :], AX.X, ALU.max))
                link(dve.tensor_scalar(mm[:, 0, :].bitcast(F32R), mx[:, :], -1.0, None, ALU.mult))
                dve.scalar_tensor_tensor(mm[:, 1, :], mx[:, :], -1.0, mm[:, 0, :], ALU.mult, ALU.subtract) \
                    .then_inc(sem["v_m"], 1)
                dve.wait_ge(sem["p_shift"], n("p_shift", 1))
                dve.tensor_copy(mt[:, :], E[0:2 * HG * RT, 0:P]).then_inc(sem["v_shift"], 1)

            def recip(n, c, k):
                dve.wait_ge(sem["a_heads"], n("a_heads"))
                half = slice(k * W // 2, (k + 1) * W // 2)
                dve.reciprocal(denom[:, half], denom[:, half]).then_inc(sem["v_recip"], 1)

            def scaled(n, c):
                dve.wait_ge(sem["v_recip"], n("v_recip"))
                dve.tensor_tensor(heads[:, :], heads[:, :], denom[:, :], ALU.mult).then_inc(sem["v_heads"], 1)

            def add(n, done, rt):
                dve.wait_ge(sem[done], n(done))
                dve.wait_ge(sem["v_dfree"], n("v_dfree"))
                d = Dk[n.dk()]
                dve.tensor_tensor(xres[:, rt, :], d[:, :], xres[:, rt, :], ALU.add).then_inc(sem["v_dfree"], 1)

            def add_wo(n, c, i):
                add(n, "p_wo", c * TPC + i)

            def add_down(n, j, blk, i, nfc):
                add(n, "p_down", blk * TPC + i)

            def gated(n, j, blk, fc, nfc):
                t = tt[:, (blk * nfc + fc) % 2, :]
                dve.wait_ge(sem["a_tanh"], n("a_tanh"))
                dve.scalar_tensor_tensor(t, t, 1.0, G[:, :], ALU.add, ALU.mult).then_inc(sem["v_gate"], 1)
                dve.wait_ge(sem["v_gate"], n("v_gate", 1))
                dve.wait_ge(sem["p_up"], n("p_up"))
                dve.scalar_tensor_tensor(t, t, both_s[:, chunk(n, j, fc)] if n.layer else 0.5, U[:, :],
                                         ALU.mult, ALU.mult).then_inc(sem["v_h"], 1)

            walk(dve, dict(v_weights=v_weights, stats=stats, xn=xn_, norm=norm, proj=proj, rotate=rotate, nat=nat, shift=shift,
                           recip=recip, scaled=scaled, add_wo=add_wo, add_down=add_down, gated=gated))

        @block.tensor
        def _(pe):
            pe.wait_ge(s_const, 8)
            pe.wait_ge(s_vconst, 2)

            def three(dst, terms, k=0, parts=1):
                seq = [m for (ah_, al_), (bh, bl) in terms for m in ((ah_, bh), (ah_, bl), (al_, bh))]
                size = len(seq) // parts
                for i in range(k * size, (k + 1) * size):
                    a, b_ = seq[i]
                    ins = pe.matmul(dst, a, b_, start=i == 0, stop=i == len(seq) - 1)
                return ins

            def norm(n, rt):
                pe.wait_ge(sem["v_xn"], n("v_xn", -1 if rt % TPC < TPC - 1 else 0))
                pe.wait_ge(sem["v_dfree"], n("v_dfree", -1))
                d = Dk[n.dk()]
                for c in range(KC):
                    ins = pe.transpose(d[:, c * P:(c + 1) * P], xn[:, rt % 2, c * P:(c + 1) * P], ident[:, :])
                ins.then_inc(sem["p_xt"], 1)

            def values(n, rt, behind):
                if rt == 0:
                    pe.wait_ge(sem["g_wv"], n("g_wv"))
                pe.wait_ge(sem["v_dfree"], n("v_dfree", -behind))
                if rt < 2:
                    pe.wait_ge(sem["a_heads"], n("a_heads"))
                else:
                    pe.wait_ge(sem["a_val"], n("a_val", -1))
                rows = slice(rt * P, (rt + 1) * P)
                three((O, E)[rt % 2][:, :], [((xh[:, c, rows], xl[:, c, rows]), (wvh[:, c, :], wvl[:, c, :]))
                                             for c in range(KC)]).then_inc(sem["p_v"], 1)

            def proj(n, t):
                if t == 0:
                    pe.wait_ge(sem["g_lo"], n.ready("A"))
                if n.region[:4] == "open":
                    pe.wait_ge(sem["v_dfree"], n("v_dfree"))
                if t < 2:
                    pe.wait_ge(sem["a_exp"], n("a_exp"))
                else:
                    if n.region[:4] == "open":
                        pe.wait_ge(sem["v_swap"], n("v_swap", -1))
                    else:
                        pe.wait_ge(sem["a_heads"], n("a_heads"))
                cols = slice((t % NC) * W, (t % NC + 1) * W)
                qk = 1 - t // NC
                three(proj_bank(n, t)[:, :], [((wqkh[:, qk, c, :], wqkl[:, qk, c, :]), (xh[:, c, cols], xl[:, c, cols]))
                                       for c in range(KC)]).then_inc(sem["p_proj"], 1)

            def nat(n, h, u):
                if u == 0:
                    pe.wait_ge(sem[f"d_stack{h}"], n(f"d_stack{h}"))
                if h == 0 and u < 4:
                    pe.wait_ge(sem["a_heads"], n("a_heads"))
                    pe.wait_ge(sem["a_val"], n("a_val"))
                else:
                    pe.wait_ge(sem["v_max"], n("v_max", -3))
                qb, part, w_ = NAT[u]
                k0 = part * W
                diag = qb * P - k0
                s = NB[(h * len(NAT) + u) % 4]
                wide = max(w_, 2 * P)
                masked = diag == w_ - P
                ins = pe.matmul(s[:, 0:wide], QS[0:STACK, h, qb * P:(qb + 1) * P], KS[0:STACK, h, k0:k0 + wide],
                                start=True, stop=not masked)
                if masked:
                    ins = pe.matmul(s[:, diag:diag + P], ident_b[:, :], mask_q[:, :], start=False, stop=True)
                ins.then_inc(sem["p_nat"], 1)

            def shift(n):
                pe.wait_ge(sem["v_m"], n("v_m", 1))
                pe.transpose(E[:, 0:P], mm[:, :, :].rearrange("p a b -> p (a b)"), ident[:, :]) \
                    .then_inc(sem["p_shift"], 1)

            def st_(n, i, h):
                c, kb = SETS[i]
                if i == 0 and h == 0:
                    pe.wait_ge(sem["d_shift"], n("d_shift"))
                skip = max(0, kb - TPC * c) * P
                first = min(skip, W - 2 * P)
                if i or h >= 2:
                    pe.wait_ge(sem["a_exp"], n("a_exp", -1))
                masked = kb >= TPC * c
                s = S[h % 2]
                ins = pe.matmul(s[:, first:W], KS[0:SHIFT, h, kb * P:(kb + 1) * P],
                                QS[0:SHIFT, h, c * W + first:(c + 1) * W], start=True, stop=not masked)
                if masked:
                    ins = pe.matmul(s[:, skip:skip + P], ident_b[:, :], mask_k[:, :], start=False, stop=True)
                ins.then_inc(sem["p_st"], 1)

            def pv(n, i):
                c, kb = SETS[i]
                skip = max(0, kb - TPC * c) * P
                if i == 0:
                    pe.wait_ge(sem["d_v"], n("d_v"))
                if kb == 0:
                    pe.wait_ge(sem["a_heads"], n("a_heads"))
                pe.wait_ge(sem["a_exp"], n("a_exp", -2 if i < len(SETS) - 1 else 0))
                for h in range(HG):
                    pe.matmul(O[h * DH:(h + 1) * DH, skip:W], vh[:, kb, h * DH:(h + 1) * DH],
                              pr[:, (i * HG + h) % 8, skip:W], start=kb == 0, stop=kb == TPC * (c + 1) - 1)

            def sums(n, i):
                c, kb = SETS[i]
                skip = max(0, kb - TPC * c) * P
                for h in range(HG):
                    ins = pe.matmul(E[h * DH:(h + 1) * DH, skip:W], ones[:, :], pr[:, (i * HG + h) % 8, skip:W],
                                    start=kb == 0, stop=kb == TPC * (c + 1) - 1)
                ins.then_inc(sem["p_pv"], 1)

            def wo_(n, c, i):
                if c == 0 and i == 0:
                    pe.wait_ge(sem["g_lo"], n.ready("O"))
                if i == 0:
                    pe.wait_ge(sem["g_al"], n("g_al"))
                pe.wait_ge(sem["v_dfree"], n("v_dfree", -1))
                rows = slice(i * P, (i + 1) * P)
                three(Dk[n.dk()][:, :], [((ah[:, rows], al[:, rows]), (woh[:, :], wol[:, :]))]) \
                    .then_inc(sem["p_wo"], 1)

            def gate_up(n, kind, j, blk, fc, k):
                wh, wl, dst, w_kind, free = {"gate": (wgh, wgl, G, "G", "v_gate"), "up": (wuh, wul, U, "U", "v_h")}[kind]
                if k == 0 and blk == 0 and fc == 0:
                    pe.wait_ge(sem["g_lo"], n.ready(w_kind))
                if k == 0:
                    pe.wait_ge(sem[free], n(free))
                cols = slice(blk * W, (blk + 1) * W)
                return three(dst[:, :], [((wh[:, fc, c, :], wl[:, fc, c, :]), (xh[:, c, cols], xl[:, c, cols]))
                                         for c in range(KC)], k, GU_PARTS)

            def gate(n, j, blk, fc, nfc):
                gate_up(n, "gate", j, blk, fc, GU_PARTS - 1).then_inc(sem["p_gate"], 1)

            def up(n, j, blk, fc, nfc):
                gate_up(n, "up", j, blk, fc, GU_PARTS - 1).then_inc(sem["p_up"], 1)

            def down(n, j, blk, i, nfc):
                if blk == 0 and i == 0:
                    pe.wait_ge(sem["g_lo"], n.ready("D"))
                if i == 0:
                    pe.wait_ge(sem["g_hl"], n("g_hl"))
                pe.wait_ge(sem["v_dfree"], n("v_dfree", -1))
                three(Dk[n.dk()][:, :], [((hh[:, fc, i * P:(i + 1) * P], hl[:, fc, i * P:(i + 1) * P]),
                                          (wdh[:, fc, :], wdl[:, fc, :])) for fc in range(nfc)]) \
                    .then_inc(sem["p_down"], 1)

            walk(pe, dict(norm=norm, values=values, proj=proj, nat=nat, shift=shift, st=st_, pv=pv, sums=sums, wo=wo_,
                          gate=gate, up=up, part=gate_up, down=down))


def chunks(w):
    return w.reshape(-1, P, KC, P).transpose(0, 3, 2, 1)


def pairs_apart(w):
    return w.reshape(H, 2, DH // 2, D).transpose(0, 2, 1, 3).reshape(D, D)


def kernel(**inputs):
    import numpy as np
    import concourse.bacc as bacc
    from concourse.bass_utils import run_bass_kernel_spmd as run

    a = {k: np.asarray(v) for k, v in inputs.items()}
    qk = [(a["L0_attn_Wq"], a["L0_attn_Wk"]), (pairs_apart(a["L1_attn_Wq"]), pairs_apart(a["L1_attn_Wk"]))]
    wqk = np.concatenate([np.stack([chunks(q), chunks(k)], axis=2) for q, k in qk]).reshape(2 * NG, P, -1)
    wo = np.concatenate([a[f"L{i}_attn_Wo"].T.reshape(NG, P, D) for i in range(2)])
    wv = np.stack([a[f"L{i}_attn_Wv"].T.reshape(KC, P, D).transpose(1, 0, 2).reshape(P, -1) for i in range(2)])
    wgate = np.concatenate([chunks(a["L0_ffn_w_gate"]), chunks(a["L1_ffn_gate_w"])]).reshape(-1, P, D)
    wup = np.concatenate([chunks(a["L0_ffn_w_up"]), chunks(a["L1_ffn_up_w"])]).reshape(-1, P, D)
    wdown = np.concatenate([a["L0_ffn_w_down"].T, a["L1_ffn_down_w"].T]).reshape(-1, P, D)
    wqk, wo = (np.concatenate([w, w[:2]]) for w in (wqk, wo))
    wgate, wup, wdown = (np.concatenate([w, w[:4]]) for w in (wgate, wup, wdown))
    scales = np.stack([a[f"L1_ffn_{g}_s"].reshape(-1, P).T for g in ("gate", "up")], axis=2)
    down_s = np.repeat(a["L1_ffn_down_s"].reshape(1, D), P, axis=0)
    half = np.arange(DH // 2, dtype=np.float32)
    theta = [np.float32(10000.0) ** (np.float32(-2.0) * half / np.float32(DH)),
             np.float32(1.0) / np.float32(10000.0) ** (half / np.float32(DH // 2))]
    rope = np.zeros((2, P, 2, T), np.float32)
    for i in range(2):
        angle = np.arange(T, dtype=np.float32)[None, :] * theta[i][:, None]
        for p in range(P):
            k = p % DH
            rope[i, p, 0] = np.cos(angle[k // 2])
            rope[i, p, 1] = np.sin(angle[k // 2]) if k % 2 else -np.sin(angle[k // 2])

    x = np.concatenate([a["L0_attn_X"], a["L0_attn_X"][:1]])
    arrays = {"x": x, "wqk": wqk, "wo": wo, "wv": wv, "wgate": wgate, "wup": wup, "wdown": wdown,
              "rope": rope, "scales": scales, "down_s": down_s}
    arrays = {f"in_{k}_dram": np.ascontiguousarray(v) for k, v in arrays.items()}
    nc = bacc.Bacc("TRN2", target_bir_lowering=False, num_devices=1)
    nc.disable_value_cache = True
    args = [nc.dram_tensor(k, v.shape, mybir.dt.from_np(v.dtype), kind="ExternalInput").ap()
            for k, v in arrays.items()]
    args.append(nc.dram_tensor("out_dram", (B, T, D), F32, kind="ExternalOutput").ap())
    two_layers(nc, *args)
    return run(nc, [arrays], core_ids=[0]).results[0]["out_dram"]
```
